# Optimizing a Trainium2 kernel written in Bass

```python
import numpy as np
import jax
import jax.numpy as jnp

def _softmax(x, axis=-1):
    return jax.nn.softmax(x, axis=axis)

def _gelu(x):
    return jax.nn.gelu(x, approximate=True)

def _silu(x):
    return jax.nn.silu(x)

def _sigmoid(x):
    return jax.nn.sigmoid(x)

def _layernorm(x, axis=-1, eps=1e-05):
    m = jnp.mean(x, axis=axis, keepdims=True)
    v = jnp.var(x, axis=axis, keepdims=True)
    return (x - m) / jnp.sqrt(v + eps)

def _scatter_add(tgt, idx, src, axis=0):
    return tgt.at[idx].add(src)

def _segment_sum(src, seg, n):
    return jax.ops.segment_sum(src, seg, n)
kernel_name = 'mk_xattn_ffn_d1_seqx_r4_563f42'

def setup_inputs(seed: int=0):
    np.random.seed(seed)
    _w = jnp.asarray

    def _rec_inputs():
        import jax
        import jax.numpy as jnp
        _rk = jax.random.key(seed)
        x = -0.0002928 + 1 * jax.random.normal(jax.random.fold_in(_rk, 1), (8, 256, 256), jnp.float32)
        _lenS = 256 - jax.random.randint(jax.random.fold_in(_rk, 7), (8,), 0, max(1, 256 // 4) + 1, jnp.int32)
        _lenS2 = 256 - jax.random.randint(jax.random.fold_in(_rk, 8), (8,), 0, max(1, 256 // 4) + 1, jnp.int32)
        _ctx_1024P = jax.random.normal(jax.random.fold_in(_rk, 11), (8, 16, 256), jnp.float32)
        _ctx_1024c = jax.random.dirichlet(jax.random.fold_in(_rk, 511), 0.3 * jnp.ones((16,), jnp.float32), (8, 256))
        _ctx_1024t = jnp.einsum('bsk,bkd->bsd', _ctx_1024c, _ctx_1024P)
        _ctx_1024t = _ctx_1024t * jax.lax.rsqrt(jnp.mean(jnp.square(_ctx_1024t)) + 1e-12) * 0.953939
        ctx_1024 = -1.39393e-06 + 0.999914 * (_ctx_1024t + 0.3 * jax.random.normal(jax.random.fold_in(_rk, 611), (8, 256, 256), jnp.float32))
        return (x, ctx_1024)
    x, ctx_1024 = _rec_inputs()

    def _L0_xattn_setup():
        import jax, jax.numpy as jnp
        import numpy as np
        B, S, D, NH = (2, 512, 256, 8)
        DH = D // NH
        EPS = 1e-06
        LN_EPS = 1e-05

        def _mlstm_cell(q, k, v, igate_w, igate_b, fgate_w, fgate_b, ln_scale):
            Slen = q.shape[0]
            ifg = jnp.concatenate([q, k, v], axis=-1)
            ig = (ifg @ igate_w.T + igate_b).T
            fg = (ifg @ fgate_w.T + fgate_b).T
            qh = q.reshape(Slen, NH, DH).transpose(1, 0, 2)
            kh = k.reshape(Slen, NH, DH).transpose(1, 0, 2)
            vh = v.reshape(Slen, NH, DH).transpose(1, 0, 2)
            log_f = jax.nn.log_sigmoid(fg)
            cs = jnp.cumsum(log_f, axis=1)
            fg_mat = cs[:, :, None] - cs[:, None, :]
            mask = jnp.tril(jnp.ones((Slen, Slen), dtype=bool))
            log_fg_mat = jnp.where(mask, fg_mat, -jnp.inf)
            log_D = log_fg_mat + ig[:, None, :]
            max_log_D = jnp.max(log_D, axis=-1, keepdims=True)
            D_mat = jnp.exp(log_D - max_log_D)
            qk = jnp.einsum('hsd,htd->hst', qh, kh) / np.sqrt(DH)
            C = qk * D_mat
            normalizer = jnp.maximum(jnp.abs(C.sum(axis=-1, keepdims=True)), jnp.exp(-max_log_D))
            h = jnp.einsum('hst,htd->hsd', C / (normalizer + EPS), vh)
            h = h.transpose(1, 0, 2).reshape(Slen, D)
            mu = h.mean(axis=-1, keepdims=True)
            var = h.var(axis=-1, keepdims=True)
            return (h - mu) / jnp.sqrt(var + LN_EPS) * ln_scale
        key = jax.random.key(seed)
        ks = jax.random.split(key, 8)
        rnd = lambda k, sh, s=1.0: jax.random.normal(k, sh, dtype=jnp.float32) * s
        return {'q': rnd(ks[0], (B, S, D)), 'k': rnd(ks[1], (B, S, D)), 'v': rnd(ks[2], (B, S, D)), 'igate_w': rnd(ks[3], (NH, 3 * D), 0.02), 'igate_b': jnp.linspace(3.0, 6.0, NH, dtype=jnp.float32), 'fgate_w': rnd(ks[4], (NH, 3 * D), 0.02), 'fgate_b': rnd(ks[5], (NH,), 0.3162278), 'ln_scale': jnp.ones((D,), dtype=jnp.float32)}
    _L0_xattn_all = _L0_xattn_setup()
    _L0_xattn_in = {k: v for k, v in _L0_xattn_all.items() if k in ('igate_w', 'igate_b', 'fgate_w', 'fgate_b', 'ln_scale')}
    del _L0_xattn_all

    def _L0_ffn_setup():
        import jax, jax.numpy as jnp
        import numpy as np
        E = 8
        K = 2
        CAP_FACTOR = 1.0
        key = jax.random.key(seed)
        ks = jax.random.split(key, 5)
        B, T, C, H = (4, 512, 256, 1024)
        x = jax.random.normal(ks[0], (B, T, C), dtype=jnp.float32)
        Wr = jax.random.normal(ks[1], (C, E), dtype=jnp.float32) * 0.02
        br = jnp.zeros((E,), jnp.float32)
        W1 = jax.random.normal(ks[2], (E, C, H), dtype=jnp.float32) * 0.02
        b1 = jnp.zeros((E, H), jnp.float32)
        W2 = jax.random.normal(ks[3], (E, H, C), dtype=jnp.float32) * 0.02
        b2 = jnp.zeros((E, C), jnp.float32)
        return {'x': x, 'Wr': Wr, 'br': br, 'W1': W1, 'b1': b1, 'W2': W2, 'b2': b2}
    _L0_ffn_all = _L0_ffn_setup()
    _L0_ffn_in = {k: v for k, v in _L0_ffn_all.items() if k in ('Wr', 'br', 'W1', 'b1', 'W2', 'b2')}
    del _L0_ffn_all
    return {'x': x, 'ctx_1024': ctx_1024, 'L0_xattn_igate_w': _L0_xattn_in['igate_w'], 'L0_xattn_igate_b': _L0_xattn_in['igate_b'], 'L0_xattn_fgate_w': _L0_xattn_in['fgate_w'], 'L0_xattn_fgate_b': _L0_xattn_in['fgate_b'], 'L0_xattn_ln_scale': _L0_xattn_in['ln_scale'], 'L0_ffn_Wr': _L0_ffn_in['Wr'], 'L0_ffn_br': _L0_ffn_in['br'], 'L0_ffn_W1': _L0_ffn_in['W1'], 'L0_ffn_b1': _L0_ffn_in['b1'], 'L0_ffn_W2': _L0_ffn_in['W2'], 'L0_ffn_b2': _L0_ffn_in['b2']}

def reference(x, ctx_1024, L0_xattn_igate_w, L0_xattn_igate_b, L0_xattn_fgate_w, L0_xattn_fgate_b, L0_xattn_ln_scale, L0_ffn_Wr, L0_ffn_br, L0_ffn_W1, L0_ffn_b1, L0_ffn_W2, L0_ffn_b2):
    import jax
    import jax.numpy as jnp

    def _L0_xattn_ref(q, k, v, igate_w, igate_b, fgate_w, fgate_b, ln_scale):
        import jax, jax.numpy as jnp
        import numpy as np
        B, S, D, NH = (2, 512, 256, 8)
        DH = D // NH
        EPS = 1e-06
        LN_EPS = 1e-05

        def _mlstm_cell(q, k, v, igate_w, igate_b, fgate_w, fgate_b, ln_scale):
            Slen = q.shape[0]
            ifg = jnp.concatenate([q, k, v], axis=-1)
            ig = (ifg @ igate_w.T + igate_b).T
            fg = (ifg @ fgate_w.T + fgate_b).T
            qh = q.reshape(Slen, NH, DH).transpose(1, 0, 2)
            kh = k.reshape(Slen, NH, DH).transpose(1, 0, 2)
            vh = v.reshape(Slen, NH, DH).transpose(1, 0, 2)
            log_f = jax.nn.log_sigmoid(fg)
            cs = jnp.cumsum(log_f, axis=1)
            fg_mat = cs[:, :, None] - cs[:, None, :]
            mask = jnp.tril(jnp.ones((Slen, Slen), dtype=bool))
            log_fg_mat = jnp.where(mask, fg_mat, -jnp.inf)
            log_D = log_fg_mat + ig[:, None, :]
            max_log_D = jnp.max(log_D, axis=-1, keepdims=True)
            D_mat = jnp.exp(log_D - max_log_D)
            qk = jnp.einsum('hsd,htd->hst', qh, kh) / np.sqrt(DH)
            C = qk * D_mat
            normalizer = jnp.maximum(jnp.abs(C.sum(axis=-1, keepdims=True)), jnp.exp(-max_log_D))
            h = jnp.einsum('hst,htd->hsd', C / (normalizer + EPS), vh)
            h = h.transpose(1, 0, 2).reshape(Slen, D)
            mu = h.mean(axis=-1, keepdims=True)
            var = h.var(axis=-1, keepdims=True)
            return (h - mu) / jnp.sqrt(var + LN_EPS) * ln_scale
        return jax.vmap(lambda qq, kk, vv: _mlstm_cell(qq, kk, vv, igate_w, igate_b, fgate_w, fgate_b, ln_scale))(q, k, v)

    def _L0_ffn_ref(x, Wr, br, W1, b1, W2, b2):
        import jax, jax.numpy as jnp
        import numpy as np
        E = 8
        K = 2
        CAP_FACTOR = 1.0
        B, T, C = x.shape
        N = B * T
        xf = x.reshape(N, C)
        logits = xf @ Wr + br
        topv, topi = jax.lax.top_k(logits, K)
        gates = jax.nn.softmax(topv, axis=-1)
        rw = jnp.zeros((N, E), xf.dtype).at[jnp.arange(N)[:, None], topi].set(gates)
        cap = int(N * K / E * CAP_FACTOR)
        sel = jax.nn.one_hot(topi, E, dtype=jnp.int32).sum(1)
        rank = jnp.cumsum(sel, axis=0) - sel
        keep = (sel > 0) & (rank < cap)
        tok = jnp.broadcast_to(jnp.arange(N, dtype=jnp.int32)[:, None], (N, E))
        eid = jnp.broadcast_to(jnp.arange(E, dtype=jnp.int32)[None, :], (N, E))
        rank_c = jnp.where(keep, rank, cap)
        buf = jnp.full((E, cap), N, dtype=jnp.int32)
        buf = buf.at[eid, rank_c].set(tok, mode='drop')
        xpad = jnp.concatenate([xf, jnp.zeros((1, C), xf.dtype)], axis=0)
        xg = xpad[buf]
        h = jax.nn.gelu(jnp.einsum('ecd,edh->ech', xg, W1) + b1[:, None, :], approximate=False)
        out = jnp.einsum('ech,ehd->ecd', h, W2) + b2[:, None, :]
        rw_pad = jnp.concatenate([rw, jnp.zeros((1, E), rw.dtype)], axis=0)
        w = rw_pad[buf, jnp.arange(E, dtype=jnp.int32)[:, None]]
        weighted = out * w[..., None]
        final = jnp.zeros((N + 1, C), xf.dtype).at[buf.reshape(-1)].add(weighted.reshape(-1, C))
        return final[:N].reshape(B, T, C)
    x = x + _L0_xattn_ref(_layernorm(x, axis=-1), ctx_1024, ctx_1024, L0_xattn_igate_w, L0_xattn_igate_b, L0_xattn_fgate_w, L0_xattn_fgate_b, L0_xattn_ln_scale)
    x = x + _L0_ffn_ref(_layernorm(x, axis=-1), L0_ffn_Wr, L0_ffn_br, L0_ffn_W1, L0_ffn_b1, L0_ffn_W2, L0_ffn_b2)
    return x

_drawn_inputs = setup_inputs


def setup_inputs(seed=0):
    import zlib

    import numpy as np

    out = dict(_drawn_inputs(seed))
    spreads = {'L0_xattn_ln_scale': (1.0, 0.2),
     'L0_ffn_br': (0.0, 0.1),
     'L0_ffn_b1': (0.0, 0.563),
     'L0_ffn_b2': (0.0, 0.1)}
    factors = {}
    for name, (base, spread) in spreads.items():
        noise = np.random.default_rng([zlib.crc32(name.encode()), seed]).standard_normal(out[name].shape)
        drawn = base * np.exp(spread * noise) if base else spread * noise
        out[name] = jnp.asarray(drawn.astype(out[name].dtype))
    for name, factor in factors.items():
        out[name] = (out[name] * factor).astype(out[name].dtype)
    return out
```

```python
from contextlib import ExitStack

import concourse.bass as bass
from concourse import mybir

ALU = mybir.AluOpType
ACT = mybir.ActivationFunctionType
AX_X = mybir.AxisListType.X
F32 = mybir.dt.float32
F32R = mybir.dt.float32r
BF16 = mybir.dt.bfloat16
U32 = mybir.dt.uint32

P = 128
MASKED = -1.0e30
DROPPED = 1.0e6
LN_EPS = 1e-5
NORM_EPS = 1e-6


class Link:

    def __init__(self, engine, sem):
        self.engine, self.sem, self.n = engine, sem, 0

    def __call__(self, instruction):
        instruction.then_inc(self.sem, 1)
        self.n += 1
        self.engine.wait_ge(self.sem, self.n)


def build_program(nc, x, ctx, igate_w, igate_b, fgate_w, fgate_b, ln_scale, Wr, br, W1, b1, W2, b2, out):
    NBATCH, S, D = x.shape
    NH = igate_w.shape[0]
    DH = D // NH
    E, _, HID = W1.shape
    N = NBATCH * S
    NT = N // P
    HALVES = S // P
    KC = D // P
    HPC = P // DH
    BH = NBATCH * NH
    CAP = N * 2 // E
    TT = CAP // P
    HJ = HID // P
    DV = DH + 1
    SCALE = float(DH) ** -0.5
    LDG = 4
    NG = NT // LDG
    ROW = D + 4
    TOKEN, FIRST, GATE = D, D + 1, D + 2
    WPIECE = 2 * HID // 4
    PIECES = 2 * KC * HID // WPIECE
    assert HALVES == 2 and KC == 2 and BH == 64 and PIECES == HJ == 8 and TT == 4

    x_t = x.rearrange("b (i p) d -> p (b i) d", p=P)
    ctx_t = ctx.rearrange("b (i p) d -> p (b i) d", p=P)
    out_t = out.rearrange("b (i p) d -> p (b i) d", p=P)
    out_rows = out.rearrange("b s d -> (b s) d")
    slots = nc.dram_tensor("slots", [E * CAP, ROW], F32).ap()
    parts = nc.dram_tensor("parts", [3, 2, BH, S], BF16).ap()

    both = ExitStack()
    with both:
        def sem(name):
            return both.enter_context(nc.semaphore(name))

        def sb(name, shape, dt, stack=both):
            return stack.enter_context(nc.sbuf_tensor(name, shape, dt))

        def psum(name, shape):
            return both.enter_context(nc.psum_tensor(name, shape, F32))

        ps_s = psum("ps_s", [P, 1024])
        ps_a = psum("ps_a", [P, 1024])
        ps_o = psum("ps_o", [P, 512])
        ps_f = psum("ps_f", [P, 512])
        ps_x = psum("ps_x", [P, 1024])
        ps_t, ps_r = ps_x[:, 0:512], ps_x[:, 512:1024]

        ident = sb("ident", [P, P], F32)
        b1_cols = sb("b1_cols", [P, E * HJ], F32)
        w_raw = sb("w_raw", [P, PIECES, WPIECE], F32)
        w_hi = [sb("w_hi0", [P, PIECES, WPIECE], F32R)]
        w_lo = [sb("w_lo0", [P, PIECES, WPIECE], F32R)]

        first = ExitStack()
        x_all = sb("x_all", [P, NT, D], F32, first)
        c_all = sb("c_all", [P, NT, D], F32, first)
        v_aug = sb("v_aug", [P, NT, NH, DV], F32, first)
        xcT = sb("xcT", [P, NT, 2 * KC, P], F32, first)
        rows_l = sb("rows_l", [P, BH // 4 * S], BF16, first)
        rows_r = sb("rows_r", [P, BH // 4 * S], BF16, first)
        q_diag = sb("q_diag", [P, 2, KC, HPC, P], F32, first)
        kdec = sb("kdec", [P, 2, D], F32, first)
        state = sb("state", [P, 2, KC, HPC * DV], F32, first)
        o_sb = sb("o_sb", [P, 2, NH * DV], F32, first)
        f_sb = sb("f_sb", [P, NH * DV], F32, first)
        h_sb = sb("h_sb", [P, 2, 2, D], F32, first)
        row = sb("row", [P, 4, 2, ROW], F32, first)
        rowT = sb("rowT", [P, KC, 2 * P], F32, first)
        pad_row = sb("pad_row", [P, ROW], F32, first)
        identb = sb("identb", [P, P], BF16, first)
        mask = sb("mask", [P, 4 * P], BF16, first)
        tri = sb("tri", [P, P], F32, first)
        stri = sb("stri", [P, P], F32, first)
        ones = sb("ones", [P, P], F32, first)
        last_row = sb("last_row", [P, P], F32, first)
        gw_q = sb("gw_q", [P, KC, 2 * NH], F32, first)
        gw_v = sb("gw_v", [P, KC, 2 * NH], F32, first)
        gw_c = sb("gw_c", [P, KC, 2 * NH], F32, first)
        gate_b = sb("gate_b", [P, 2 * NH], F32, first)
        lns = sb("lns", [P, D], F32, first)
        br_b = sb("br_b", [P, E], F32, first)
        wr_sb = sb("wr_sb", [P, KC, E], F32, first)
        eps_half = sb("eps_half", [P, LDG], F32, first)
        gates = sb("gates", [P, NT, 2 * NH], F32, first)
        csum = sb("csum", [P, 2, BH], F32, first)
        acol = sb("acol", [P, 2, BH], F32, first)
        mtok = sb("mtok", [P, 2, BH], F32, first)
        floor_n = sb("floor_n", [P, 2, BH], F32, first)
        qfac = sb("qfac", [P, BH], F32, first)
        kfac = sb("kfac", [P, BH], F32, first)
        mv_x = sb("mv_x", [P, NT, 2], F32, first)
        rs_x = sb("rs_x", [P, NT], F32, first)
        stat = sb("stat", [P, 2, 6], F32, first)
        stat_1 = sb("stat_1", [P, 2, 6], F32, first)
        mv_h = sb("mv_h", [P, 2, 2], F32, first)
        rs_h = sb("rs_h", [P, 2], F32, first)
        mv_1 = sb("mv_1", [P, 2, 2], F32, first)
        rs_1 = sb("rs_1", [P, 2], F32, first)
        den = sb("den", [P, 2, NH], F32, first)
        iota_e = sb("iota_e", [P, E], F32, first)
        token_id = sb("token_id", [P, NT], U32, first)
        logits = sb("logits", [P, 2, E], F32, first)
        top = sb("top", [P, 2, 8], F32, first)
        topi = sb("topi", [P, 2, 8], U32, first)
        topf = sb("topf", [P, 2, 2], F32, first)
        hot = sb("hot", [P, 2, 2, E], F32, first)
        sel = sb("sel", [P, 2, E], F32, first)
        before = sb("before", [P, NT + 1, E], F32, first)
        gdiff = sb("gdiff", [P, 2], F32, first)
        gexp = sb("gexp", [P, 2], F32, first)
        hotrank = sb("hotrank", [P, 2, 2, E], F32, first)
        rank = sb("rank", [P, 2, 2], F32, first)
        over = sb("over", [P, 2, 2], F32, first)
        slot_f = sb("slot_f", [P, 2, 2], F32, first)
        slot_i = sb("slot_i", [P, 2, 4], U32, first)
        early = ExitStack()
        xn = sb("xn", [P, LDG, D], F32, early)
        gw = sb("gw", [2 * NH, 3 * D], F32, early)
        b1_raw = sb("b1_raw", [E * HJ, P], F32, early)
        fabs = sb("fabs", [P, NT, NH], F32, early)
        logf = sb("logf", [P, NT, NH], F32, early)
        am = sb("am", [BH, 2, S], F32, early)
        mrow = sb("mrow", [BH, S], F32, early)
        part = [sb(f"part{k}", [BH, 2, S], BF16, early) for k in range(3)]
        stat_x = sb("stat_x", [P, NT, 6], F32, early)
        early.close()
        decay = sb("decay", [P, 2, NH * P], F32, first)
        cmat = sb("cmat", [P, 2, NH * P], F32, first)
        first.close()

        w_hi.append(sb("w_hi1", [P, PIECES, WPIECE], F32R))
        w_lo.append(sb("w_lo1", [P, PIECES, WPIECE], F32R))
        xg = sb("xg", [P, 2, TT, ROW], F32)
        x_hi = sb("x_hi", [P, 2, KC, CAP], F32R)
        x_lo = sb("x_lo", [P, 2, KC, CAP], F32R)
        g_f = sb("g_f", [P, 3, CAP], F32)
        g_hi = sb("g_hi", [P, 3, CAP], F32R)
        g_lo = sb("g_lo", [P, 3, CAP], F32R)
        acc = sb("acc", [P, TT, D], F32)
        bias_w = sb("bias_w", [P, TT, D], F32)
        res = sb("res", [P, TT, D], F32)
        b2_b = sb("b2_b", [P, 2, D], F32)
        gate_w = sb("gate_w", [P, 2, TT], F32)
        gate_2 = sb("gate_2", [P, 2, TT], F32)

        dve_link, pool_link, act_link = sem("dve_link"), sem("pool_link"), sem("act_link")
        x_in = [sem(f"x_in{g}") for g in range(NG)]
        c_in = [sem(f"c_in{g}") for g in range(NG)]
        small_in = sem("small_in")
        consts = sem("consts")
        gw_turned, gw_ready = sem("gw_turned"), sem("gw_ready")
        x_stats, x_rstd, xn_ready = sem("x_stats"), sem("x_rstd"), sem("xn_ready")
        xc_turned, xc_copied = sem("xc_turned"), sem("xc_copied")
        gates_done, fabs_ready, softplus_ready = sem("gates_done"), sem("fabs_ready"), sem("softplus_ready")
        logf_ready, csum_done, acol_ready = sem("logf_ready"), sem("csum_done"), sem("acol_ready")
        a_turned, a_copied, m_scanned = sem("a_turned"), sem("a_copied"), sem("m_scanned")
        m_turned, mtok_ready, ref_ready = sem("m_turned"), sem("mtok_ready"), sem("ref_ready")
        exps_in, factors_ready = sem("exps_in"), sem("factors_ready")
        parts_ready, parts_out, rows_in, rows_set = sem("parts_ready"), sem("parts_out"), sem("rows_in"), sem("rows_set")
        v_ready, kdec_ready = sem("v_ready"), sem("kdec_ready")
        pad_ready, pads_out = sem("pad_ready"), sem("pads_out")
        log_done, exp_done, q_ready, s_done, c_ready, o_done = (
            sem("log_done"), sem("exp_done"), sem("q_ready"), sem("s_done"), sem("c_ready"), sem("o_done"))
        state_done, state_ready, f_done, o_taken = sem("state_done"), sem("state_ready"), sem("f_done"), sem("o_taken")
        h_stats, h_rstd, h_normed, x1_ready = sem("h_stats"), sem("h_rstd"), sem("h_normed"), sem("x1_ready")
        x1_out, x1_stats, x1_rstd, row_ready = sem("x1_out"), sem("x1_stats"), sem("x1_rstd"), sem("row_ready")
        row_turned, rowT_ready = sem("row_turned"), sem("rowT_ready")
        router_done, picked, gexp_ready, placed = sem("router_done"), sem("picked"), sem("gexp_ready"), sem("placed")
        rows_out = [sem("rows_out0"), sem("rows_out1")]
        w_in = [sem(f"w_in{j}") for j in range(PIECES)]
        w_hi_ready, w_lo_ready = sem("w_hi_ready"), sem("w_lo_ready")
        xg_in = [sem("xg_in0"), sem("xg_in1")]
        b2_in = [sem("b2_in0"), sem("b2_in1")]
        xg_turned, x_hi_ready, x_lo_ready = sem("xg_turned"), sem("x_hi_ready"), sem("x_lo_ready")
        ffn1_done, gelu_done, g_hi_ready, g_lo_ready = sem("ffn1_done"), sem("gelu_done"), sem("g_hi_ready"), sem("g_lo_ready")
        ffn2_done, res_ready, weights_ready = sem("ffn2_done"), sem("res_ready"), sem("weights_ready")
        w_phase = sem("w_phase")
        acc_set, acc_in, acc_ready, res_out = sem("acc_set"), sem("acc_in"), sem("acc_ready"), sem("res_out")

        UNITS = NT
        STEPS = UNITS + 9
        NSMALL = 8

        def batch_at(step, lag):
            b = (step - lag) // 2
            return b if (step - lag) % 2 == 0 and 0 <= b < NBATCH else None

        def turn_bank(t):
            bank = (ps_s, ps_s, ps_a, ps_a)[t % 4]
            return bank[:, (t % 2) * 512:(t % 2 + 1) * 512]

        def out_bank(t):
            return (ps_a[:, 0:D], ps_a[:, 512:512 + D], ps_o[:, 0:D], ps_f[:, 0:D])[t]

        block = both.enter_context(nc.Block())

        @block.sync
        def _(sp):
            for g in range(NG):
                sp.dma_start(x_all[:, g * LDG:(g + 1) * LDG, :], x_t[:, g * LDG:(g + 1) * LDG, :]).then_inc(x_in[g], 16)
                sp.dma_start(c_all[:, g * LDG:(g + 1) * LDG, :], ctx_t[:, g * LDG:(g + 1) * LDG, :]).then_inc(c_in[g], 16)
            sp.wait_ge(pad_ready, 1)
            sp.dma_start(slots.rearrange("(t p) r -> p t r", p=P),
                         pad_row[:, :].rearrange("p (a r) -> p a r", a=1).broadcast_to([P, E * TT, ROW])).then_inc(pads_out, 16)

            def load_piece(e, j):
                if e >= 1:
                    sp.wait_ge(w_lo_ready, (e - 1) * PIECES + j + 1)
                if j < PIECES // 2:
                    k, half = j // 2, j % 2
                    src = W1[e, k * P:(k + 1) * P, half * WPIECE:(half + 1) * WPIECE]
                    sp.dma_start(w_raw[:, j, :], src).then_inc(w_in[j], 16)
                else:
                    c = 2 * (j - PIECES // 2)
                    src = W2[e, c * P:(c + 2) * P, :].rearrange("(a p) d -> p a d", p=P)
                    sp.dma_start(w_raw[:, j, :].rearrange("p (a d) -> p a d", a=2), src).then_inc(w_in[j], 16)

            for k in range(3):
                sp.wait_ge(parts_ready, k + 1)
                sp.dma_start(parts[k].rearrange("w q s -> q w s"), part[k][:, :, :]).then_inc(parts_out, 16)
            sp.wait_ge(parts_out, 48)
            sp.wait_ge(rows_set, 2)
            q = BH // 4
            for r in range(4):
                sp.dma_start(rows_r[32 * r:32 * r + 3, :],
                             parts[:, 1, r * q:(r + 1) * q, :].rearrange("k q s -> k (q s)")).then_inc(rows_in, 16)
                sp.dma_start(rows_l[32 * r + 3:32 * r + 6, :],
                             parts[:, 0, r * q:(r + 1) * q, :].rearrange("k q s -> k (q s)")).then_inc(rows_in, 16)
            for j in range(PIECES):
                load_piece(0, j)
            for b in range(NBATCH):
                sp.wait_ge(x1_ready, b + 1)
                sp.dma_start(out_t[:, 2 * b:2 * b + 2, :], x_all[:, 2 * b:2 * b + 2, :]).then_inc(x1_out, 16)

            def load_expert(e):
                if e >= 2:
                    sp.wait_ge(xg_turned, e - 1)
                    sp.wait_ge(weights_ready, e - 1)
                    sp.wait_ge(res_out, 16 * TT * (e - 1))
                sp.dma_start(xg[:, e % 2, :, :], slots[e * CAP:(e + 1) * CAP, :].rearrange("(t p) r -> p t r", p=P)
                             ).then_inc(xg_in[e % 2], 16)
                if e >= 2:
                    sp.wait_ge(acc_ready, TT * (e - 1))
                sp.dma_start(b2_b[:, e % 2, :], b2[e:e + 1, :].broadcast_to([P, D])).then_inc(b2_in[e % 2], 16)

            for s in range(2):
                sp.wait_ge(rows_out[s], 64 * NBATCH // 2)
            load_expert(0)
            load_expert(1)
            for e in range(1, E):
                for j in range(PIECES):
                    load_piece(e, j)
                if e >= 2:
                    load_expert(e)

        @block.gpsimd
        def _(pool):
            link = Link(pool, pool_link)
            nc.gpsimd.memset(eps_half[:, :], -0.5)
            link(nc.gpsimd.memset(ident[:, :], 0.0))
            link(nc.gpsimd.affine_select(out=ident[:, :], in_=ident[:, :], compare_op=ALU.not_equal, fill=1.0,
                                         base=0, pattern=[[-1, P]], channel_multiplier=1))
            nc.gpsimd.memset(ones[:, :], 1.0).then_inc(consts, 1)

            def rstd_x(g):
                sl = slice(g * LDG, (g + 1) * LDG)
                pool.wait_ge(x_stats, g + 1)
                link(nc.gpsimd.tensor_scalar(rs_x[:, sl], mv_x[:, sl, 1], LN_EPS, None, ALU.add))
                nc.gpsimd.tensor_tensor(rs_x[:, sl], rs_x[:, sl], eps_half[:, 0:LDG], ALU.pow).then_inc(x_rstd, 1)

            rstd_x(0)
            nc.gpsimd.memset(tri[:, :], 1.0)
            nc.gpsimd.memset(stri[:, :], 1.0)
            nc.gpsimd.memset(last_row[:, :], 0.0)
            nc.gpsimd.memset(mask[:, :], 0.0)
            link(nc.gpsimd.memset(pad_row[:, :], 0.0))
            nc.gpsimd.affine_select(out=tri[:, :], in_=tri[:, :], compare_op=ALU.is_ge, fill=0.0,
                                    base=0, pattern=[[1, P]], channel_multiplier=-1)
            nc.gpsimd.affine_select(out=stri[:, :], in_=stri[:, :], compare_op=ALU.is_gt, fill=0.0,
                                    base=0, pattern=[[1, P]], channel_multiplier=-1)
            rstd_x(1)
            nc.gpsimd.affine_select(out=last_row[:, :], in_=last_row[:, :], compare_op=ALU.not_equal, fill=1.0,
                                    base=1 - P, pattern=[[0, P]], channel_multiplier=1)
            nc.gpsimd.affine_select(out=mask[:, :], in_=mask[:, :], compare_op=ALU.is_ge, fill=MASKED,
                                    base=0, pattern=[[0, 4], [1, P]], channel_multiplier=-1)
            nc.gpsimd.tensor_copy(identb[:, :], ident[:, :])
            nc.gpsimd.iota(pad_row[:, TOKEN:TOKEN + 1].bitcast(U32), pattern=[[0, 1]], base=int(DROPPED),
                           channel_multiplier=0).then_inc(pad_ready, 1)
            nc.gpsimd.iota(token_id[:, :], pattern=[[P, NT]], base=0, channel_multiplier=1)
            nc.gpsimd.iota(iota_e[:, :], pattern=[[1, E]], base=0, channel_multiplier=0,
                           allow_small_or_imprecise_dtypes=True)
            nc.gpsimd.memset(before[:, 0, :], 0.0).then_inc(consts, 1)
            rstd_x(2)
            nc.gpsimd.memset(rows_l[:, :], 1.0).then_inc(rows_set, 1)
            rstd_x(3)
            nc.gpsimd.memset(rows_r[:, :], 1.0).then_inc(rows_set, 1)
            nc.gpsimd.memset(state[:, :, :, :], 0.0)
            nc.gpsimd.memset(q_diag[:, :, :, :, :], 0.0).then_inc(consts, 1)
            link(nc.gpsimd.memset(v_aug[:, :, :, DH:DV], 1.0))
            for g in range(NG):
                pool.wait_ge(c_in[g], 16)
                for t in range(g * LDG, (g + 1) * LDG):
                    nc.gpsimd.tensor_copy(v_aug[:, t, :, 0:DH], c_all[:, t, :].rearrange("p (h d) -> p h d", h=NH)
                                          ).then_inc(v_ready, 1)

            def decayed_keys(b):
                if b >= 2:
                    pool.wait_ge(state_done, b - 1)
                if b == 0:
                    pool.wait_ge(factors_ready, 1)
                nc.gpsimd.tensor_tensor(kdec[:, b % 2, :].rearrange("p (h d) -> p h d", h=NH),
                                        c_all[:, 2 * b, :].rearrange("p (h d) -> p h d", h=NH),
                                        kfac[:, b * NH:(b + 1) * NH].unsqueeze(2).broadcast_to([P, NH, DH]),
                                        ALU.mult).then_inc(kdec_ready, 1)

            decayed_keys(0)
            for step in range(STEPS + 1):
                if (b := batch_at(step, -1)) is not None or (b := batch_at(step, -2)) is not None:
                    if step % 2 == 1:
                        decayed_keys(b)
                if (b := batch_at(step, 2)) is not None:
                    pool.wait_ge(h_stats, b + 1)
                    link(nc.gpsimd.tensor_scalar(rs_h[:, :], mv_h[:, :, 1], LN_EPS, None, ALU.add))
                    nc.gpsimd.tensor_tensor(rs_h[:, :], rs_h[:, :], eps_half[:, 0:2], ALU.pow).then_inc(h_rstd, 1)
                if (b := batch_at(step, 3)) is not None:
                    hh = h_sb[:, b % 2, :, :]
                    pool.wait_ge(h_normed, b + 1)
                    link(nc.gpsimd.tensor_tensor(hh, hh, lns[:, :].unsqueeze(1).broadcast_to([P, 2, D]), ALU.mult))
                    x1 = x_all[:, 2 * b:2 * b + 2, :]
                    nc.gpsimd.tensor_tensor(x1, hh, x1, ALU.add).then_inc(x1_ready, 1)
                if (b := batch_at(step, 4)) is not None:
                    pool.wait_ge(x1_stats, b + 1)
                    link(nc.gpsimd.tensor_scalar(rs_1[:, :], mv_1[:, :, 1], LN_EPS, None, ALU.add))
                    nc.gpsimd.tensor_tensor(rs_1[:, :], rs_1[:, :], eps_half[:, 0:2], ALU.pow).then_inc(x1_rstd, 1)
                if (b := batch_at(step, 10)) is not None:
                    pool.wait_ge(placed, b + 1)
                    if b == 0:
                        pool.wait_ge(pads_out, 16)
                    for i in range(2):
                        for k in range(2):
                            c = 2 * i + k
                            nc.gpsimd.indirect_dma_start(
                                slots, bass.IndirectOffsetOnAxis(ap=slot_i[:, b % 2, c:c + 1], axis=0),
                                row[:, b % 4, i, :], None, bounds_check=E * CAP - 1, oob_is_err=False,
                            ).then_inc(rows_out[b % 2], 16)

            pool.wait_ge(w_phase, 1)
            nc.gpsimd.memset(acc[:, :, :], 0.0).then_inc(acc_set, 1)
            pool.wait_ge(acc_set, 1)
            pool.wait_ge(x1_out, 16 * NBATCH)
            for e in range(E):
                pool.wait_ge(xg_in[e % 2], 16 * (e // 2 + 1))
                pool.wait_ge(b2_in[e % 2], 16 * (e // 2 + 1))
                if e >= 1:
                    pool.wait_ge(res_out, 16 * TT * e)
                    pool.wait_ge(res_ready, TT * e)
                for t in range(TT):
                    nc.gpsimd.indirect_dma_start(
                        acc[:, t, :], None, out_rows,
                        bass.IndirectOffsetOnAxis(ap=xg[:, e % 2, t, TOKEN:TOKEN + 1].bitcast(U32), axis=0),
                        bounds_check=N - 1, oob_is_err=False).then_inc(acc_in, 16)
                pool.wait_ge(weights_ready, e + 1)
                for t in range(TT):
                    last = nc.gpsimd.tensor_scalar(bias_w[:, t, :], b2_b[:, e % 2, :], gate_w[:, e % 2, t:t + 1], None, ALU.mult)
                link(last)
                pool.wait_ge(acc_in, 16 * TT * (e + 1))
                for t in range(TT):
                    nc.gpsimd.tensor_tensor(acc[:, t, :], acc[:, t, :], bias_w[:, t, :], ALU.add).then_inc(acc_ready, 1)
                for t in range(TT):
                    pool.wait_ge(res_ready, TT * e + t + 1)
                    nc.gpsimd.indirect_dma_start(
                        out_rows, bass.IndirectOffsetOnAxis(ap=xg[:, e % 2, t, TOKEN:TOKEN + 1].bitcast(U32), axis=0),
                        res[:, t, :], None, bounds_check=N - 1, oob_is_err=False).then_inc(res_out, 16)
            pool.wait_ge(res_out, 16 * TT * E)

        @block.scalar
        def _(act):
            link = Link(act, act_link)
            act.dma_start(gw[0:NH, :], igate_w).then_inc(small_in, 16)
            act.dma_start(gw[NH:2 * NH, :], fgate_w).then_inc(small_in, 16)
            act.dma_start(gate_b[:, 0:NH], igate_b.rearrange("(a n) -> a n", a=1).broadcast_to([P, NH])).then_inc(small_in, 16)
            act.dma_start(gate_b[:, NH:2 * NH], fgate_b.rearrange("(a n) -> a n", a=1).broadcast_to([P, NH])).then_inc(small_in, 16)
            act.dma_start(b1_raw[:, :], b1.rearrange("e (j p) -> (e j) p", p=P)).then_inc(small_in, 16)
            act.dma_start(wr_sb[:, :, :], Wr.rearrange("(k p) e -> p k e", p=P)).then_inc(small_in, 16)
            act.dma_start(lns[:, :], ln_scale.rearrange("(a n) -> a n", a=1).broadcast_to([P, D])).then_inc(small_in, 16)
            act.dma_start(br_b[:, :], br.rearrange("(a n) -> a n", a=1).broadcast_to([P, E])).then_inc(small_in, 16)
            for t in range(NT):
                act.wait_ge(xc_turned, t + 1)
                nc.scalar.activation(xcT[:, t, :, :], turn_bank(t), ACT.Copy).then_inc(xc_copied, 1)
            act.wait_ge(fabs_ready, 1)
            link(nc.scalar.activation(fabs[:, :, :], fabs[:, :, :], ACT.Exp, scale=-1.0))
            nc.scalar.activation(fabs[:, :, :], fabs[:, :, :], ACT.Ln, bias=1.0).then_inc(softplus_ready, 1)
            act.wait_ge(a_turned, 1)
            nc.scalar.activation(am[:, 0, :], ps_s[0:BH, 0:S], ACT.Copy).then_inc(a_copied, 1)
            act.wait_ge(exps_in, 1)
            nc.scalar.activation(floor_n[:, :, :], floor_n[:, :, :], ACT.Exp, scale=-1.0)
            nc.scalar.activation(qfac[:, :], qfac[:, :], ACT.Exp)
            nc.scalar.activation(kfac[:, :], kfac[:, :], ACT.Exp).then_inc(factors_ready, 1)

            def diag_queries(u):
                if u == 0:
                    act.wait_ge(consts, 3)
                if u >= 2:
                    act.wait_ge(s_done, u - 1)
                for j in range(HPC):
                    last = nc.scalar.activation(q_diag[DH * j:DH * (j + 1), u % 2, :, j, :],
                                                xcT[DH * j:DH * (j + 1), u, 0:KC, :], ACT.Copy)
                    last.then_inc(q_ready, 1)

            diag_queries(0)
            for step in range(STEPS + 1):
                if step < UNITS:
                    act.wait_ge(log_done, step + 1)
                    if step >= 2:
                        act.wait_ge(c_ready, step - 1)
                    nc.scalar.activation(decay[:, step % 2, :], ps_a[:, :], ACT.Exp).then_inc(exp_done, 1)
                if step + 1 < UNITS:
                    diag_queries(step + 1)
                if (b := batch_at(step, 0)) is not None:
                    act.wait_ge(state_done, b + 1)
                    if b >= 2:
                        act.wait_ge(f_done, b - 1)
                    for j in range(HPC):
                        nc.scalar.activation(
                            state[DH * j:DH * (j + 1), b % 2, :, DV * j:DV * (j + 1)],
                            ps_f[DH * j:DH * (j + 1), 0:KC * HPC * DV].rearrange("p (k n) -> p k n", k=KC)[:, :, DV * j:DV * (j + 1)],
                            ACT.Copy).then_inc(state_ready, 1)
                if (b := batch_at(step, 7)) is not None:
                    act.wait_ge(row_turned, b + 1)
                    if b >= 1:
                        act.wait_ge(router_done, b)
                    nc.scalar.activation(rowT[:, :, :], ps_t.rearrange("p (k s) -> p k s", k=KC), ACT.Copy).then_inc(rowT_ready, 1)
                if (b := batch_at(step, 8)) is not None:
                    act.wait_ge(picked, b + 1)
                    nc.scalar.activation(gexp[:, :], gdiff[:, :], ACT.Exp).then_inc(gexp_ready, 1)
                if step in (20, 22):
                    for j in range(4 * (step // 2 - 10), 4 * (step // 2 - 10) + 4):
                        act.wait_ge(w_in[j], 16)
                        nc.scalar.activation(w_hi[0][:, j, :], w_raw[:, j, :], ACT.Copy).then_inc(w_hi_ready, 1)

            def x_high(e):
                act.wait_ge(xg_turned, e + 1)
                if e >= 2:
                    act.wait_ge(ffn1_done, HJ * (e - 1))
                nc.scalar.activation(x_hi[:, e % 2, :, :], ps_x[:, :].rearrange("p (k s) -> p k s", k=KC), ACT.Copy
                                     ).then_inc(x_hi_ready, 1)

            x_high(0)
            for g in range(E * HJ):
                e, j = divmod(g, HJ)
                act.wait_ge(ffn1_done, g + 1)
                if g >= 3:
                    act.wait_ge(g_lo_ready, g - 2)
                nc.scalar.activation(g_f[:, g % 3, :], ps_s[:, (g % 2) * CAP:(g % 2 + 1) * CAP], ACT.Gelu,
                                     bias=b1_cols[:, g:g + 1]).then_inc(gelu_done, 1)
                if e + 1 < E:
                    act.wait_ge(w_in[j], 16 * (e + 2))
                    if e >= 1:
                        act.wait_ge(ffn1_done, HJ * e) if j < 4 else act.wait_ge(ffn2_done, HJ * e)
                    nc.scalar.activation(w_hi[(e + 1) % 2][:, j, :], w_raw[:, j, :], ACT.Copy).then_inc(w_hi_ready, 1)
                act.wait_ge(gelu_done, g + 1)
                if g >= 3:
                    act.wait_ge(ffn2_done, g - 2)
                nc.scalar.activation(g_hi[:, g % 3, :], g_f[:, g % 3, :], ACT.Copy).then_inc(g_hi_ready, 1)
                if j == 5 and e + 1 < E:
                    x_high(e + 1)

        @block.vector
        def _(dve):
            link = Link(dve, dve_link)
            for g in range(NG):
                dve.wait_ge(x_in[g], 16)
                tiles = range(g * LDG, (g + 1) * LDG)
                for t in tiles:
                    last = nc.vector.bn_stats(stat_x[:, t, :], x_all[:, t, :])
                link(last)
                for t in tiles:
                    last = nc.vector.bn_aggr(mv_x[:, t, :], stat_x[:, t, :])
                last.then_inc(x_stats, 1)
                if g == 0:
                    dve.wait_ge(gw_turned, 1)
                    w = 2 * NH
                    nc.vector.tensor_copy(gw_q[:, :, :], ps_t[:, 0:2 * w].rearrange("p (k n) -> p k n", k=KC))
                    nc.vector.tensor_copy(b1_cols[:, :], ps_t[:, 6 * w:6 * w + E * HJ])
                    link(nc.vector.tensor_copy(gw_v[:, :, :], ps_t[:, 4 * w:6 * w].rearrange("p (k n) -> p k n", k=KC)))
                    nc.vector.tensor_tensor(gw_c[:, :, :], ps_t[:, 2 * w:4 * w].rearrange("p (k n) -> p k n", k=KC),
                                            gw_v[:, :, :], ALU.add).then_inc(gw_ready, 1)
                dve.wait_ge(x_rstd, g + 1)
                for t in tiles:
                    if t >= LDG:
                        dve.wait_ge(xc_turned, t - LDG + 1)
                    nc.vector.tensor_scalar(xn[:, t % LDG, :], x_all[:, t, :], mv_x[:, t, 0:1], rs_x[:, t:t + 1],
                                            ALU.subtract, ALU.mult).then_inc(xn_ready, 1)
            dve.wait_ge(gates_done, 1)
            dve.wait_ge(small_in, 16 * NSMALL)
            link(nc.vector.tensor_tensor(gates[:, :, :], ps_r[:, 0:NT * 2 * NH].rearrange("p (t n) -> p t n", t=NT),
                                         gate_b[:, :].unsqueeze(1).broadcast_to([P, NT, 2 * NH]), ALU.add))
            nc.vector.scalar_tensor_tensor(out=fabs[:, :, :], in0=gates[:, :, NH:2 * NH], scalar=-1.0,
                                           in1=gates[:, :, NH:2 * NH], op0=ALU.mult, op1=ALU.max).then_inc(fabs_ready, 1)
            dve.wait_ge(softplus_ready, 1)
            nc.vector.scalar_tensor_tensor(out=logf[:, :, :], in0=gates[:, :, NH:2 * NH], scalar=0.0, in1=fabs[:, :, :],
                                           op0=ALU.min, op1=ALU.subtract).then_inc(logf_ready, 1)
            dve.wait_ge(csum_done, 1)
            for i in range(2):
                last = nc.vector.tensor_copy(csum[:, i, :].rearrange("p (b h) -> p b h", b=NBATCH),
                                             ps_t[:, 0:NT * NH].rearrange("p (b i h) -> p b i h", i=2, h=NH)[:, :, i, :])
            link(last)
            for i in range(2):
                last = nc.vector.tensor_tensor(acol[:, i, :].rearrange("p (b h) -> p b h", b=NBATCH),
                                               gates[:, :, 0:NH].rearrange("p (b i) h -> p b i h", i=2)[:, :, i, :],
                                               csum[:, i, :].rearrange("p (b h) -> p b h", b=NBATCH), ALU.subtract)
            last.then_inc(acol_ready, 1)
            dve.wait_ge(a_copied, 1)
            nc.vector.tensor_tensor_scan(mrow[:, :], am[:, 0, :], am[:, 0, :], -3.0e38, ALU.max, ALU.max).then_inc(m_scanned, 1)
            dve.wait_ge(m_scanned, 1)
            link(nc.vector.tensor_scalar(am[:, 1, :], mrow[:, :], -1.0, None, ALU.mult))
            for k in range(3):
                nc.vector.tensor_copy(part[k][:, :, :], am[:, :, :]).then_inc(parts_ready, 1)
                dve.wait_ge(parts_ready, k + 1)
                if k < 2:
                    link(nc.vector.tensor_tensor(am[:, :, :], am[:, :, :], part[k][:, :, :], ALU.subtract))
            dve.wait_ge(m_turned, 1)
            link(nc.vector.tensor_copy(mtok[:, :, :], ps_s[:, 0:2 * BH].rearrange("p (i n) -> p i n", i=2)))
            nc.vector.tensor_tensor(floor_n[:, :, :], csum[:, :, :], mtok[:, :, :], ALU.add).then_inc(mtok_ready, 1)
            dve.wait_ge(ref_ready, 1)
            nc.vector.tensor_tensor(qfac[:, :], ps_o[:, 0:BH], mtok[:, 1, :], ALU.subtract)
            nc.vector.scalar_tensor_tensor(out=kfac[:, :], in0=ps_o[:, 0:BH], scalar=-1.0, in1=acol[:, 0, :],
                                           op0=ALU.mult, op1=ALU.add).then_inc(exps_in, 1)

            for step in range(STEPS + 1):
                if step < UNITS:
                    u = step
                    dve.wait_ge(s_done, u + 1)
                    dve.wait_ge(exp_done, u + 1)
                    if u >= 2:
                        dve.wait_ge(o_done, u - 1)
                    nc.vector.tensor_tensor(cmat[:, u % 2, :], ps_s[:, :], decay[:, u % 2, :], ALU.mult).then_inc(c_ready, 1)
                u = step - 1
                if 0 <= u < UNITS:
                    b, i = divmod(u, 2)
                    dve.wait_ge(o_done, u + 1)
                    if i == 0:
                        nc.vector.tensor_copy(o_sb[:, 0, :], ps_o[:, 0:NH * DV]).then_inc(o_taken, 1)
                    else:
                        if b == 0:
                            dve.wait_ge(factors_ready, 1)
                        dve.wait_ge(f_done, b + 1)
                        link(nc.vector.tensor_tensor(f_sb[:, :].rearrange("p (h n) -> p h n", h=NH),
                                                     ps_f[:, 0:NH * DV].rearrange("p (h n) -> p h n", h=NH),
                                                     qfac[:, b * NH:(b + 1) * NH].unsqueeze(2).broadcast_to([P, NH, DV]),
                                                     ALU.mult))
                        nc.vector.tensor_tensor(o_sb[:, 1, :], ps_o[:, 0:NH * DV], f_sb[:, :], ALU.add).then_inc(o_taken, 1)
                if (b := batch_at(step, 2)) is not None:
                    hh = h_sb[:, b % 2, :, :]
                    osb = o_sb[:, :, :].rearrange("p i (h n) -> p i h n", h=NH)
                    fl = floor_n[:, :, b * NH:(b + 1) * NH]
                    dve.wait_ge(o_taken, 2 * b + 2)
                    link(nc.vector.scalar_tensor_tensor(out=den[:, :, :], in0=osb[:, :, :, DH], scalar=-1.0,
                                                        in1=osb[:, :, :, DH], op0=ALU.mult, op1=ALU.max))
                    link(nc.vector.scalar_tensor_tensor(out=den[:, :, :], in0=den[:, :, :], scalar=SCALE, in1=fl,
                                                        op0=ALU.mult, op1=ALU.max))
                    link(nc.vector.tensor_scalar(den[:, :, :], den[:, :, :], NORM_EPS, 1.0 / SCALE, ALU.add, ALU.mult))
                    link(nc.vector.reciprocal(den[:, :, :], den[:, :, :]))
                    if b >= 2:
                        dve.wait_ge(x1_ready, b - 1)
                    for i in range(2):
                        last = nc.vector.tensor_tensor(hh[:, i, :].rearrange("p (h d) -> p h d", h=NH), osb[:, i, :, 0:DH],
                                                       den[:, i, :].unsqueeze(2).broadcast_to([P, NH, DH]), ALU.mult)
                    link(last)
                    for i in range(2):
                        last = nc.vector.bn_stats(stat[:, i, :], hh[:, i, :])
                    link(last)
                    for i in range(2):
                        last = nc.vector.bn_aggr(mv_h[:, i, :], stat[:, i, :])
                    last.then_inc(h_stats, 1)
                if (b := batch_at(step, 3)) is not None:
                    hh = h_sb[:, b % 2, :, :]
                    dve.wait_ge(h_rstd, b + 1)
                    for i in range(2):
                        last = nc.vector.tensor_scalar(hh[:, i, :], hh[:, i, :], mv_h[:, i, 0:1], rs_h[:, i:i + 1],
                                                       ALU.subtract, ALU.mult)
                    last.then_inc(h_normed, 1)
                if (b := batch_at(step, 4)) is not None:
                    dve.wait_ge(x1_ready, b + 1)
                    for i in range(2):
                        last = nc.vector.bn_stats(stat_1[:, i, :], x_all[:, 2 * b + i, :])
                    link(last)
                    for i in range(2):
                        last = nc.vector.bn_aggr(mv_1[:, i, :], stat_1[:, i, :])
                    last.then_inc(x1_stats, 1)
                if (b := batch_at(step, 5)) is not None:
                    dve.wait_ge(x1_rstd, b + 1)
                    if b >= 4:
                        dve.wait_ge(rows_out[b % 2], 64 * (b // 2 - 1))
                    for i in range(2):
                        last = nc.vector.tensor_scalar(row[:, b % 4, i, 0:D], x_all[:, 2 * b + i, :], mv_1[:, i, 0:1],
                                                       rs_1[:, i:i + 1], ALU.subtract, ALU.mult)
                    last.then_inc(row_ready, 1)
                if (b := batch_at(step, 10)) is not None:
                    dve.wait_ge(router_done, min(b + 2, NBATCH + 1))
                    link(nc.vector.tensor_tensor(hotrank[:, :, :, :], hot[:, :, :, :],
                                                 ps_r[:, 64:64 + 2 * E].rearrange("p (i e) -> p i e", i=2).unsqueeze(2)
                                                 .broadcast_to([P, 2, 2, E]), ALU.mult))
                    link(nc.vector.tensor_reduce(rank[:, :, :], hotrank[:, :, :, :], AX_X, ALU.add))
                    nc.vector.tensor_scalar(over[:, :, :], rank[:, :, :], float(CAP), DROPPED, ALU.is_ge, ALU.mult)
                    link(nc.vector.scalar_tensor_tensor(out=slot_f[:, :, :], in0=topf[:, :, :], scalar=float(CAP),
                                                        in1=rank[:, :, :], op0=ALU.mult, op1=ALU.add))
                    if b >= 2:
                        dve.wait_ge(rows_out[b % 2], 64 * (b // 2))
                    nc.vector.tensor_tensor(slot_i[:, b % 2, :].rearrange("p (i k) -> p i k", i=2), slot_f[:, :, :],
                                            over[:, :, :], ALU.add)
                    dve.wait_ge(gexp_ready, b + 1)
                    rw = row[:, b % 4, :, :]
                    link(nc.vector.tensor_scalar(gdiff[:, :], gexp[:, :], 1.0, None, ALU.add))
                    link(nc.vector.reciprocal(rw[:, :, GATE], gdiff[:, :]))
                    nc.vector.tensor_tensor(rw[:, :, GATE + 1], gexp[:, :], rw[:, :, GATE], ALU.mult)
                    nc.vector.tensor_copy(rw[:, :, FIRST], topf[:, :, 0])
                    nc.vector.tensor_copy(rw[:, :, TOKEN].bitcast(U32), token_id[:, 2 * b:2 * b + 2]).then_inc(placed, 1)
                if (b := batch_at(step, 8)) is not None:
                    dve.wait_ge(router_done, b + 1)
                    if b >= 1:
                        dve.wait_ge(gexp_ready, b)
                        dve.wait_ge(placed, b)
                    link(nc.vector.tensor_tensor(logits[:, :, :], ps_r[:, 0:2 * E].rearrange("p (i e) -> p i e", i=2),
                                                 br_b[:, :].unsqueeze(1).broadcast_to([P, 2, E]), ALU.add))
                    for i in range(2):
                        last = nc.vector.max(top[:, i, :], logits[:, i, :])
                    link(last)
                    for i in range(2):
                        last = nc.vector.max_index(topi[:, i, :], top[:, i, :], logits[:, i, :])
                    nc.vector.tensor_tensor(gdiff[:, :], top[:, :, 1], top[:, :, 0], ALU.subtract)
                    link(last)
                    link(nc.vector.tensor_copy(topf[:, :, :], topi[:, :, 0:2]))
                    link(nc.vector.tensor_tensor(hot[:, :, :, :],
                                                 iota_e[:, :].unsqueeze(1).unsqueeze(1).broadcast_to([P, 2, 2, E]),
                                                 topf[:, :, :].unsqueeze(3).broadcast_to([P, 2, 2, E]), ALU.is_equal))
                    link(nc.vector.tensor_tensor(sel[:, :, :], hot[:, :, 0, :], hot[:, :, 1, :], ALU.add))
                    link(nc.vector.tensor_tensor(before[:, 2 * b + 1, :], before[:, 2 * b, :], sel[:, 0, :], ALU.add))
                    nc.vector.tensor_tensor(before[:, 2 * b + 2, :], before[:, 2 * b + 1, :], sel[:, 1, :], ALU.add
                                            ).then_inc(picked, 1)
                if step in (20, 22):
                    for j in range(4 * (step // 2 - 10), 4 * (step // 2 - 10) + 4):
                        dve.wait_ge(w_hi_ready, j + 1)
                        nc.vector.tensor_tensor(w_lo[0][:, j, :], w_raw[:, j, :], w_hi[0][:, j, :].bitcast(F32), ALU.subtract
                                                ).then_inc(w_lo_ready, 1)
            dve.wait_ge(placed, NBATCH)
            nc.vector.memset(gate_w[:, :, :], 0.0).then_inc(w_phase, 1)
            dve.wait_ge(w_phase, 1)

            def x_low(e):
                dve.wait_ge(x_hi_ready, e + 1)
                nc.vector.tensor_tensor(x_lo[:, e % 2, :, :], ps_x[:, :].rearrange("p (k s) -> p k s", k=KC),
                                        x_hi[:, e % 2, :, :].bitcast(F32), ALU.subtract).then_inc(x_lo_ready, 1)

            def slot_weights(e):
                s = e % 2
                dve.wait_ge(xg_in[s], 16 * (e // 2 + 1))
                nc.vector.scalar_tensor_tensor(out=gate_w[:, s, :], in0=xg[:, s, :, FIRST], scalar=float(e),
                                               in1=xg[:, s, :, GATE], op0=ALU.is_equal, op1=ALU.mult)
                link(nc.vector.scalar_tensor_tensor(out=gate_2[:, s, :], in0=xg[:, s, :, FIRST], scalar=float(e),
                                                    in1=xg[:, s, :, GATE + 1], op0=ALU.not_equal, op1=ALU.mult))
                nc.vector.tensor_tensor(gate_w[:, s, :], gate_w[:, s, :], gate_2[:, s, :], ALU.add).then_inc(weights_ready, 1)

            def results(e):
                for t in range(TT):
                    if t == 0:
                        dve.wait_ge(ffn2_done, HJ * (e + 1))
                        if e >= 1:
                            dve.wait_ge(res_out, 16 * TT * e)
                    dve.wait_ge(acc_ready, TT * e + t + 1)
                    nc.vector.scalar_tensor_tensor(out=res[:, t, :], in0=out_bank(t), scalar=gate_w[:, e % 2, t:t + 1],
                                                   in1=acc[:, t, :], op0=ALU.mult, op1=ALU.add).then_inc(res_ready, 1)

            x_low(0)
            slot_weights(0)
            for g in range(E * HJ):
                e, j = divmod(g, HJ)
                if j == 2 and e >= 1:
                    results(e - 1)
                if e + 1 < E:
                    dve.wait_ge(w_hi_ready, PIECES * (e + 1) + j + 1)
                    nc.vector.tensor_tensor(w_lo[(e + 1) % 2][:, j, :], w_raw[:, j, :], w_hi[(e + 1) % 2][:, j, :].bitcast(F32),
                                            ALU.subtract).then_inc(w_lo_ready, 1)
                dve.wait_ge(g_hi_ready, g + 1)
                if g >= 3:
                    dve.wait_ge(ffn2_done, g - 2)
                nc.vector.tensor_tensor(g_lo[:, g % 3, :], g_f[:, g % 3, :], g_hi[:, g % 3, :].bitcast(F32), ALU.subtract
                                        ).then_inc(g_lo_ready, 1)
                if j == 5 and e + 1 < E:
                    x_low(e + 1)
                    slot_weights(e + 1)
            results(E - 1)

        @block.tensor
        def _(pe):
            mm = nc.tensor.matmul
            pe.wait_ge(consts, 1)
            pe.wait_ge(small_in, 16 * NSMALL)
            w = 2 * NH
            for c in range(6):
                nc.tensor.transpose(ps_t[:, c * w:(c + 1) * w], gw[:, c * P:(c + 1) * P], ident[0:w, 0:w])
            nc.tensor.transpose(ps_t[:, 6 * w:6 * w + E * HJ], b1_raw[:, :], ident[0:E * HJ, 0:E * HJ]).then_inc(gw_turned, 1)

            def turn(t):
                pe.wait_ge(xn_ready, t + 1)
                pe.wait_ge(c_in[t // LDG], 16)
                if t >= 4:
                    pe.wait_ge(xc_copied, t - 3)
                bank = turn_bank(t)
                for k in range(KC):
                    nc.tensor.transpose(bank[:, (KC + k) * P:(KC + k + 1) * P], c_all[:, t, k * P:(k + 1) * P], ident[:, :])
                for k in range(KC):
                    last = nc.tensor.transpose(bank[:, k * P:(k + 1) * P], xn[:, t % LDG, k * P:(k + 1) * P], ident[:, :])
                last.then_inc(xc_turned, 1)

            def gate_product(t):
                pe.wait_ge(xc_copied, t + 1)
                for c in range(2 * KC):
                    rhs = gw_q[:, c, :] if c < KC else gw_c[:, c - KC, :]
                    last = mm(ps_r[:, t * w:(t + 1) * w], xcT[:, t, c, :], rhs, start=(c == 0), stop=(c == 2 * KC - 1))
                return last

            for t in range(NT):
                turn(t)
                if t == 1:
                    pe.wait_ge(gw_ready, 1)
                if t >= 1:
                    gate_product(t - 1)
            gate_product(NT - 1).then_inc(gates_done, 1)
            pe.wait_ge(logf_ready, 1)
            pe.wait_ge(consts, 2)
            mm(ps_t[:, 0:NT * NH], tri[:, :], logf[:, :, :].rearrange("p t h -> p (t h)"), start=True, stop=False,
               skip_group_check=True)
            mm(ps_t[:, 0:NT * NH].rearrange("p (b i h) -> p b i h", i=2, h=NH)[:, :, 1, :], ones[:, :],
               logf[:, :, :].rearrange("p (b i) h -> p b i h", i=2)[:, :, 0, :], start=False, stop=True,
               skip_group_check=True).then_inc(csum_done, 1)
            pe.wait_ge(acol_ready, 1)
            for i in range(2):
                last = nc.tensor.transpose(ps_s[0:BH, i * P:(i + 1) * P], acol[:, i, :], ident[:, :])
            last.then_inc(a_turned, 1)
            pe.wait_ge(m_scanned, 1)
            pe.wait_ge(a_copied, 1)
            for i in range(2):
                last = nc.tensor.transpose(ps_s[:, i * BH:(i + 1) * BH], mrow[:, i * P:(i + 1) * P], ident[0:BH, 0:BH])
            last.then_inc(m_turned, 1)
            pe.wait_ge(mtok_ready, 1)
            mm(ps_o[:, 0:BH], last_row[:, :], mtok[:, 0, :], start=True, stop=True).then_inc(ref_ready, 1)

            def log_decay(u):
                b, i = divmod(u, 2)
                if u == 0:
                    pe.wait_ge(rows_in, 16 * 8)
                if u >= 1:
                    pe.wait_ge(exp_done, u)
                for h in range(NH):
                    r, q = divmod(b * NH + h, BH // 4)
                    cols = slice(q * S + i * P, q * S + (i + 1) * P)
                    mm(ps_a[:, h * P:(h + 1) * P], rows_l[32 * r:32 * r + 6, cols], rows_r[32 * r:32 * r + 6, cols],
                       start=(h % 4 == 0), stop=False, skip_group_check=True)
                for n in range(2):
                    last = mm(ps_a[:, n * 512:(n + 1) * 512], identb[:, :], mask[:, :], start=False, stop=True,
                              skip_group_check=True)
                last.then_inc(log_done, 1)

            def scores(u):
                pe.wait_ge(q_ready, HPC * (u + 1))
                if u >= 1:
                    pe.wait_ge(c_ready, u)
                for k in range(KC):
                    last = mm(ps_s[:, k * 512:(k + 1) * 512], xcT[:, u, KC + k, :],
                              q_diag[:, u % 2, k, :, :].rearrange("p j s -> p (j s)"), start=True, stop=True)
                last.then_inc(s_done, 1)

            def attend(u):
                pe.wait_ge(c_ready, u + 1)
                if u >= 1:
                    pe.wait_ge(o_taken, u)
                for h in range(NH):
                    last = mm(ps_o[:, h * DV:(h + 1) * DV], cmat[:, u % 2, h * P:(h + 1) * P], v_aug[:, u, h, :],
                              start=True, stop=True)
                last.then_inc(o_done, 1)

            for step in range(STEPS + 1):
                if step < UNITS:
                    log_decay(step)
                if (b := batch_at(step, 7)) is not None:
                    pe.wait_ge(row_ready, b + 1)
                    if b >= 1:
                        pe.wait_ge(rowT_ready, b)
                    for k in range(KC):
                        for i in range(2):
                            last = nc.tensor.transpose(ps_t[:, (2 * k + i) * P:(2 * k + i + 1) * P],
                                                       row[:, b % 4, i, k * P:(k + 1) * P], ident[:, :])
                    last.then_inc(row_turned, 1)
                ranked, routed = batch_at(step, 10), batch_at(step, 8)
                if ranked is not None:
                    b = ranked
                    pe.wait_ge(picked, b + 1)
                    if b >= 1:
                        pe.wait_ge(placed, b)
                    for i in range(2):
                        mm(ps_r[:, 64 + i * E:64 + (i + 1) * E], stri[:, :], sel[:, i, :], start=True, stop=False)
                        last = mm(ps_r[:, 64 + i * E:64 + (i + 1) * E], ones[:, :], before[:, 2 * b + i, :], start=False, stop=True)
                if routed is not None:
                    b = routed
                    pe.wait_ge(rowT_ready, b + 1)
                    if b >= 1:
                        pe.wait_ge(picked, b)
                    for i in range(2):
                        for k in range(KC):
                            last = mm(ps_r[:, i * E:(i + 1) * E], rowT[:, k, i * P:(i + 1) * P], wr_sb[:, k, :],
                                      start=(k == 0), stop=(k == KC - 1))
                if ranked is not None or routed is not None:
                    last.then_inc(router_done, 1)
                if 0 <= step - 1 < UNITS:
                    attend(step - 1)
                if step < UNITS:
                    scores(step)
                if (b := batch_at(step, 0)) is not None:
                    pe.wait_ge(kdec_ready, b + 1)
                    pe.wait_ge(v_ready, 2 * b + 2)
                    if b >= 1:
                        pe.wait_ge(o_taken, 2 * b)
                    for k in range(KC):
                        n = HPC * DV
                        last = mm(ps_f[:, k * n:(k + 1) * n], kdec[:, b % 2, k * P:(k + 1) * P],
                                  v_aug[:, 2 * b, k * HPC:(k + 1) * HPC, :].rearrange("p h n -> p (h n)"), start=True, stop=True)
                    last.then_inc(state_done, 1)
                if (b := batch_at(step, 1)) is not None:
                    pe.wait_ge(state_ready, HPC * (b + 1))
                    for k in range(KC):
                        n = HPC * DV
                        last = mm(ps_f[:, k * n:(k + 1) * n], xcT[:, 2 * b + 1, k, :], state[:, b % 2, k, :], start=True, stop=True)
                    last.then_inc(f_done, 1)

            def turn_slots(e):
                pe.wait_ge(xg_in[e % 2], 16 * (e // 2 + 1))
                if e >= 1:
                    pe.wait_ge(x_lo_ready, e)
                else:
                    pe.wait_ge(placed, NBATCH)
                for k in range(KC):
                    for t in range(TT):
                        last = nc.tensor.transpose(ps_x[:, k * CAP + t * P:k * CAP + (t + 1) * P],
                                                   xg[:, e % 2, t, k * P:(k + 1) * P], ident[:, :])
                last.then_inc(xg_turned, 1)

            def hidden(g):
                e, j = divmod(g, HJ)
                s = e % 2
                if j == 0:
                    pe.wait_ge(w_lo_ready, PIECES * (e + 1))
                    pe.wait_ge(x_lo_ready, e + 1)
                if g >= 2:
                    pe.wait_ge(gelu_done, g - 1)
                bank = ps_s[:, (g % 2) * CAP:(g % 2 + 1) * CAP]
                n = 0
                for k in range(KC):
                    piece, at = 2 * k + j // 4, (j % 4) * P
                    hi, lo = w_hi[s][:, piece, at:at + P], w_lo[s][:, piece, at:at + P]
                    for a, b in ((hi, x_hi), (lo, x_hi), (hi, x_lo)):
                        last = mm(bank, a, b[:, s, k, :], start=(n == 0), stop=(n == 3 * KC - 1))
                        n += 1
                last.then_inc(ffn1_done, 1)

            def output(g):
                e, j = divmod(g, HJ)
                s = e % 2
                piece, at = PIECES // 2 + j // 2, (j % 2) * D
                hi, lo = w_hi[s][:, piece, at:at + D], w_lo[s][:, piece, at:at + D]
                pe.wait_ge(g_lo_ready, g + 1)
                for t in range(TT):
                    if j == 0 and e >= 1:
                        pe.wait_ge(res_ready, TT * (e - 1) + t + 1)
                    cols = slice(t * P, (t + 1) * P)
                    for n, (a, b) in enumerate(((g_hi, hi), (g_hi, lo), (g_lo, hi))):
                        last = mm(out_bank(t), a[:, g % 3, cols], b, start=(j == 0 and n == 0), stop=(j == HJ - 1 and n == 2))
                last.then_inc(ffn2_done, 1)

            turn_slots(0)
            LAG = 2
            for g in range(E * HJ + LAG):
                if g < E * HJ:
                    hidden(g)
                if g >= LAG:
                    output(g - LAG)
                if g % HJ == 5 and g // HJ + 1 < E:
                    turn_slots(g // HJ + 1)




_INS = ["x", "ctx_1024", "L0_xattn_igate_w", "L0_xattn_igate_b", "L0_xattn_fgate_w", "L0_xattn_fgate_b",
        "L0_xattn_ln_scale", "L0_ffn_Wr", "L0_ffn_br", "L0_ffn_W1", "L0_ffn_b1", "L0_ffn_W2", "L0_ffn_b2"]
_OUTS = [((8, 256, 256), "float32")]


def kernel(**inputs):
    import numpy as _np
    import concourse.bacc as _bacc
    from concourse import mybir as _mybir
    from concourse.bass_utils import run_bass_kernel_spmd as _run

    nc = _bacc.Bacc("TRN2", target_bir_lowering=False, num_devices=1)
    arrays, args = {}, []
    for name in _INS:
        a = _np.ascontiguousarray(inputs[name])
        arrays[f"in_{name}_dram"] = a
        args.append(nc.dram_tensor(f"in_{name}_dram", a.shape, _mybir.dt.from_np(a.dtype), kind="ExternalInput").ap())
    for i, (shape, dtype) in enumerate(_OUTS):
        dt = _mybir.dt.from_np(_np.dtype(dtype))
        args.append(nc.dram_tensor(f"out_{i}_dram", shape, dt, kind="ExternalOutput").ap())
    build_program(nc, *args)
    r = _run(nc, [arrays], core_ids=[0])
    got = tuple(r.results[0][f"out_{i}_dram"] for i in range(len(_OUTS)))
    return got[0]
```

```python
from contextlib import ExitStack

import concourse.bass as bass
from concourse import mybir

ALU = mybir.AluOpType
ACT = mybir.ActivationFunctionType
AX_X = mybir.AxisListType.X
F32 = mybir.dt.float32
F32R = mybir.dt.float32r
BF16 = mybir.dt.bfloat16
U32 = mybir.dt.uint32

P = 128
MASKED = -1.0e30
DROPPED = 1.0e6
LN_EPS = 1e-5
NORM_EPS = 1e-6


class Link:

    def __init__(self, engine, sem):
        self.engine, self.sem, self.n = engine, sem, 0

    def __call__(self, instruction):
        instruction.then_inc(self.sem, 1)
        self.n += 1
        self.engine.wait_ge(self.sem, self.n)


def build_program(nc, x, ctx, igate_w, igate_b, fgate_w, fgate_b, ln_scale, Wr, br, W1, b1, W2, b2, out):
    NBATCH, S, D = x.shape
    NH = igate_w.shape[0]
    DH = D // NH
    E, _, HID = W1.shape
    N = NBATCH * S
    NT = N // P
    HALVES = S // P
    KC = D // P
    HPC = P // DH
    BH = NBATCH * NH
    CAP = N * 2 // E
    TT = CAP // P
    HJ = HID // P
    DV = DH + 1
    SCALE = float(DH) ** -0.5
    OW = P // 2
    VPAD = OW - DV + 1
    LDG = 4
    NG = NT // LDG
    ROW = D + 4
    ROWS = 5
    TOKEN, FIRST, GATE = D, D + 1, D + 2
    WPIECE = 2 * HID // 4
    PIECES = 2 * KC * HID // WPIECE
    assert HALVES == 2 and KC == 2 and BH == 64 and PIECES == HJ == 8 and TT == 4

    x_t = x.rearrange("b (i p) d -> p (b i) d", p=P)
    ctx_t = ctx.rearrange("b (i p) d -> p (b i) d", p=P)
    out_t = out.rearrange("b (i p) d -> p (b i) d", p=P)
    out_rows = out.rearrange("b s d -> (b s) d")
    slots = nc.dram_tensor("slots", [E * CAP, ROW], F32).ap()
    parts = nc.dram_tensor("parts", [3, 2, BH, S], BF16).ap()

    both = ExitStack()
    with both:
        def sem(name):
            return both.enter_context(nc.semaphore(name))

        def sb(name, shape, dt, stack=both):
            return stack.enter_context(nc.sbuf_tensor(name, shape, dt))

        def psum(name, shape):
            return both.enter_context(nc.psum_tensor(name, shape, F32))

        ps_s = psum("ps_s", [P, 1024])
        ps_a = psum("ps_a", [P, 1024])
        ps_o = psum("ps_o", [P, 512])
        ps_f = psum("ps_f", [P, 512])
        ps_x = psum("ps_x", [P, 1024])
        ps_t, ps_r = ps_x[:, 0:512], ps_x[:, 512:1024]

        ident = sb("ident", [P, P], F32)
        b1_cols = sb("b1_cols", [P, E * HJ], F32)
        w_raw = sb("w_raw", [P, PIECES, WPIECE], F32)
        w_hi = [sb("w_hi0", [P, PIECES, WPIECE], F32R)]
        w_lo = [sb("w_lo0", [P, PIECES, WPIECE], F32R)]

        first = ExitStack()
        x_all = sb("x_all", [P, NT, D], F32, first)
        c_all = sb("c_all", [P, NT, D], F32, first)
        v_aug = sb("v_aug", [P, NT, NH * DV + VPAD], F32, first)
        xcT = sb("xcT", [P, NT, 2 * KC, P], F32, first)
        rows_l = sb("rows_l", [P, BH // 4 * S], BF16, first)
        rows_r = sb("rows_r", [P, BH // 4 * S], BF16, first)
        q_diag = sb("q_diag", [P, 2, KC, HPC, P], F32, first)
        kdec = sb("kdec", [P, 2, D], F32, first)
        state = sb("state", [P, 2, KC, HPC * DV], F32, first)
        oT_sb = sb("oT_sb", [P, NH * OW], F32, first)
        o_sb = sb("o_sb", [P, 2, NH * DV], F32, first)
        f_sb = sb("f_sb", [P, NH * DV], F32, first)
        h_sb = sb("h_sb", [P, 2, 2, D], F32, first)
        row = sb("row", [P, ROWS, 2, ROW], F32, first)
        rowT = sb("rowT", [P, KC, 2 * P], F32, first)
        pad_row = sb("pad_row", [P, ROW], F32, first)
        identb = sb("identb", [P, P], BF16, first)
        mask = sb("mask", [P, 4 * P], BF16, first)
        tri = sb("tri", [P, P], F32, first)
        stri = sb("stri", [P, P], BF16, first)
        ones = sb("ones", [P, P], F32, first)
        ones_b = sb("ones_b", [P, P], BF16, first)
        last_row = sb("last_row", [P, P], F32, first)
        gw_q = sb("gw_q", [P, KC, 2 * NH], F32, first)
        gw_v = sb("gw_v", [P, KC, 2 * NH], F32, first)
        gw_c = sb("gw_c", [P, KC, 2 * NH], F32, first)
        gate_b = sb("gate_b", [P, 2 * NH], F32, first)
        lns = sb("lns", [P, D], F32, first)
        br_b = sb("br_b", [P, E], F32, first)
        wr_sb = sb("wr_sb", [P, KC, E], F32, first)
        eps_half = sb("eps_half", [P, LDG], F32, first)
        gates = sb("gates", [P, NT, 2 * NH], F32, first)
        csum = sb("csum", [P, 2, BH], F32, first)
        acol = sb("acol", [P, 2, BH], F32, first)
        mtok = sb("mtok", [P, 2, BH], F32, first)
        floor_n = sb("floor_n", [P, 2, BH], F32, first)
        qfac = sb("qfac", [P, BH], F32, first)
        kfac = sb("kfac", [P, BH], F32, first)
        mv_x = sb("mv_x", [P, NT, 2], F32, first)
        rs_x = sb("rs_x", [P, NT], F32, first)
        stat = sb("stat", [P, 2, 6], F32, first)
        stat_1 = sb("stat_1", [P, 2, 6], F32, first)
        mv_h = sb("mv_h", [P, 2, 2], F32, first)
        rs_h = sb("rs_h", [P, 2], F32, first)
        mv_1 = sb("mv_1", [P, 2, 2], F32, first)
        rs_1 = sb("rs_1", [P, 2], F32, first)
        den = sb("den", [P, 2, NH], F32, first)
        iota_e = sb("iota_e", [P, E], F32, first)
        token_id = sb("token_id", [P, NT], U32, first)
        logits = sb("logits", [P, 2, E], F32, first)
        top = sb("top", [P, 2, 8], F32, first)
        topi = sb("topi", [P, 2, 8], U32, first)
        topf = sb("topf", [P, 2, 2, 2], F32, first)
        hot = sb("hot", [P, 2, 2, 2, E], F32, first)
        sel = sb("sel", [P, 2, E], BF16, first)
        before = sb("before", [P, NT + 1, E], BF16, first)
        gdiff = sb("gdiff", [P, 2, 2], F32, first)
        gexp = sb("gexp", [P, 2, 2], F32, first)
        hotrank = sb("hotrank", [P, 2, 2, E], F32, first)
        rank = sb("rank", [P, 2, 2], F32, first)
        over = sb("over", [P, 2, 2], F32, first)
        slot_f = sb("slot_f", [P, 2, 2], F32, first)
        slot_i = sb("slot_i", [P, 2, 4], U32, first)
        early = ExitStack()
        xn = sb("xn", [P, LDG, D], F32, early)
        gw = sb("gw", [2 * NH, 3 * D], F32, early)
        b1_raw = sb("b1_raw", [E * HJ, P], F32, early)
        fabs = sb("fabs", [P, NT, NH], F32, early)
        logf = sb("logf", [P, NT, NH], F32, early)
        am = sb("am", [BH, 2, S], F32, early)
        mrow = sb("mrow", [BH, S], F32, early)
        part = [sb(f"part{k}", [BH, 2, S], BF16, early) for k in range(3)]
        stat_x = sb("stat_x", [P, NT, 6], F32, early)
        gT = am[0:2 * NH, :, :].rearrange("p q s -> p (q s)")
        early.close()
        decay = sb("decay", [P, 2, NH * P], F32, first)
        cmat = sb("cmat", [P, 2, NH * P], F32, first)
        first.close()

        w_hi.append(sb("w_hi1", [P, PIECES, WPIECE], F32R))
        w_lo.append(sb("w_lo1", [P, PIECES, WPIECE], F32R))
        xg = sb("xg", [P, 2, TT, ROW], F32)
        x_hi = sb("x_hi", [P, 2, KC, CAP], F32R)
        x_lo = sb("x_lo", [P, 2, KC, CAP], F32R)
        g_f = sb("g_f", [P, 3, CAP], F32)
        g_hi = sb("g_hi", [P, 3, CAP], F32R)
        g_lo = sb("g_lo", [P, 3, CAP], F32R)
        acc = sb("acc", [P, TT, D], F32)
        bias_w = sb("bias_w", [P, TT, D], F32)
        res = sb("res", [P, TT, D], F32)
        b2_b = sb("b2_b", [P, 2, D], F32)
        gate_w = sb("gate_w", [P, 2, TT], F32)
        gate_2 = sb("gate_2", [P, 2, TT], F32)

        dve_link, pool_link, act_link = sem("dve_link"), sem("pool_link"), sem("act_link")
        x_in = [sem(f"x_in{g}") for g in range(NG)]
        c_in = [sem(f"c_in{g}") for g in range(NG)]
        small_in = sem("small_in")
        consts = sem("consts")
        gw_turned, gw_ready = sem("gw_turned"), sem("gw_ready")
        x_stats, x_rstd, xn_ready = sem("x_stats"), sem("x_rstd"), sem("xn_ready")
        xc_turned, xc_copied = sem("xc_turned"), sem("xc_copied")
        gT_done, gT_copied = sem("gT_done"), sem("gT_copied")
        gates_done, fabs_ready, softplus_ready = sem("gates_done"), sem("fabs_ready"), sem("softplus_ready")
        logf_ready, csum_done, acol_ready = sem("logf_ready"), sem("csum_done"), sem("acol_ready")
        a_turned, a_copied, m_scanned = sem("a_turned"), sem("a_copied"), sem("m_scanned")
        m_turned, mtok_ready, ref_ready = sem("m_turned"), sem("mtok_ready"), sem("ref_ready")
        exps_in, factors_ready = sem("exps_in"), sem("factors_ready")
        parts_ready, parts_out, rows_set = sem("parts_ready"), sem("parts_out"), sem("rows_set")
        rows_in = [sem(f"rows_in{r}") for r in range(4)]
        v_ready, kdec_ready = sem("v_ready"), sem("kdec_ready")
        pad_ready, pads_out = sem("pad_ready"), sem("pads_out")
        log_done, exp_done, q_ready, s_done, c_ready, o_done = (
            sem("log_done"), sem("exp_done"), sem("q_ready"), sem("s_done"), sem("c_ready"), sem("o_done"))
        oT_done, oT_copied = sem("oT_done"), sem("oT_copied")
        state_done, state_ready, f_done, o_taken = sem("state_done"), sem("state_ready"), sem("f_done"), sem("o_taken")
        f_taken, hot_ranked = sem("f_taken"), sem("hot_ranked")
        h_stats, h_rstd, h_normed, x1_ready = sem("h_stats"), sem("h_rstd"), sem("h_normed"), sem("x1_ready")
        x1_out, x1_stats, x1_rstd, row_ready = sem("x1_out"), sem("x1_stats"), sem("x1_rstd"), sem("row_ready")
        row_turned, rowT_ready = sem("row_turned"), sem("rowT_ready")
        router_done, picked, gexp_ready, placed = sem("router_done"), sem("picked"), sem("gexp_ready"), sem("placed")
        rows_out = [sem("rows_out0"), sem("rows_out1")]
        w_in = [sem(f"w_in{j}") for j in range(PIECES)]
        w_hi_ready, w_lo_ready = sem("w_hi_ready"), sem("w_lo_ready")
        xg_first = [sem(f"xg_first{t}") for t in range(TT)]
        xg_in = [sem("xg_in0"), sem("xg_in1")]
        b2_in = [sem("b2_in0"), sem("b2_in1")]
        xg_turned, x_hi_ready, x_lo_ready = sem("xg_turned"), sem("x_hi_ready"), sem("x_lo_ready")
        ffn1_done, gelu_done, g_hi_ready, g_lo_ready = sem("ffn1_done"), sem("gelu_done"), sem("g_hi_ready"), sem("g_lo_ready")
        ffn2_done, res_ready, weights_ready = sem("ffn2_done"), sem("res_ready"), sem("weights_ready")
        w_phase = sem("w_phase")
        acc_set, acc_in, acc_ready, res_out = sem("acc_set"), sem("acc_in"), sem("acc_ready"), sem("res_out")

        UNITS = NT
        STEPS = UNITS + 8
        NSMALL = 8

        def batch_at(step, lag):
            b = (step - lag) // 2
            return b if (step - lag) % 2 == 0 and 0 <= b < NBATCH else None

        def turn_bank(t):
            bank = (ps_s, ps_s, ps_a, ps_a)[t % 4]
            return bank[:, (t % 2) * 512:(t % 2 + 1) * 512]

        def gate_bank(g):
            return (ps_r, ps_o)[g % 2][0:2 * NH, 0:LDG * P]

        def out_bank(t):
            return (ps_a[:, 0:D], ps_a[:, 512:512 + D], ps_o[:, 0:D], ps_f[:, 0:D])[t]

        block = both.enter_context(nc.Block())

        @block.sync
        def _(sp):
            for g in range(NG):
                sp.dma_start(x_all[:, g * LDG:(g + 1) * LDG, :], x_t[:, g * LDG:(g + 1) * LDG, :]).then_inc(x_in[g], 16)
                sp.dma_start(c_all[:, g * LDG:(g + 1) * LDG, :], ctx_t[:, g * LDG:(g + 1) * LDG, :]).then_inc(c_in[g], 16)
            sp.wait_ge(pad_ready, 1)
            sp.dma_start(slots.rearrange("(t p) r -> p t r", p=P),
                         pad_row[:, :].rearrange("p (a r) -> p a r", a=1).broadcast_to([P, E * TT, ROW])).then_inc(pads_out, 16)

            def load_piece(e, j):
                if e >= 1:
                    sp.wait_ge(w_lo_ready, (e - 1) * PIECES + j + 1)
                if j < PIECES // 2:
                    k, half = j // 2, j % 2
                    src = W1[e, k * P:(k + 1) * P, half * WPIECE:(half + 1) * WPIECE]
                    sp.dma_start(w_raw[:, j, :], src).then_inc(w_in[j], 16)
                else:
                    c = 2 * (j - PIECES // 2)
                    src = W2[e, c * P:(c + 2) * P, :].rearrange("(a p) d -> p a d", p=P)
                    sp.dma_start(w_raw[:, j, :].rearrange("p (a d) -> p a d", a=2), src).then_inc(w_in[j], 16)

            for k in range(3):
                sp.wait_ge(parts_ready, k + 1)
                sp.dma_start(parts[k].rearrange("w q s -> q w s"), part[k][:, :, :]).then_inc(parts_out, 16)
            sp.wait_ge(parts_out, 48)
            sp.wait_ge(rows_set, 2)
            q = BH // 4
            for r in range(4):
                sp.dma_start(rows_r[32 * r:32 * r + 3, :],
                             parts[:, 1, r * q:(r + 1) * q, :].rearrange("k q s -> k (q s)")).then_inc(rows_in[r], 16)
                sp.dma_start(rows_l[32 * r + 3:32 * r + 6, :],
                             parts[:, 0, r * q:(r + 1) * q, :].rearrange("k q s -> k (q s)")).then_inc(rows_in[r], 16)
            for j in range(PIECES):
                load_piece(0, j)
            for b in range(NBATCH):
                sp.wait_ge(x1_ready, b + 1)
                sp.dma_start(out_t[:, 2 * b:2 * b + 2, :], x_all[:, 2 * b:2 * b + 2, :]).then_inc(x1_out, 16)

            def load_expert(e):
                if e >= 2:
                    sp.wait_ge(xg_turned, e - 1)
                    sp.wait_ge(weights_ready, e - 1)
                    sp.wait_ge(res_out, 16 * TT * (e - 1))
                rows = slots[e * CAP:(e + 1) * CAP, :].rearrange("(t p) r -> p t r", p=P)
                if e == 0:
                    for t in range(TT):
                        sp.dma_start(xg[:, 0, t, :], rows[:, t, :]).then_inc(xg_first[t], 16)
                else:
                    sp.dma_start(xg[:, e % 2, :, :], rows).then_inc(xg_in[e % 2], 16)
                if e >= 2:
                    sp.wait_ge(acc_ready, TT * (e - 1))
                sp.dma_start(b2_b[:, e % 2, :], b2[e:e + 1, :].broadcast_to([P, D])).then_inc(b2_in[e % 2], 16)

            for j in range(PIECES):
                load_piece(1, j)
            for s in range(2):
                sp.wait_ge(rows_out[s], 64 * NBATCH // 2)
            load_expert(0)
            load_expert(1)
            for e in range(2, E):
                for j in range(PIECES):
                    load_piece(e, j)
                load_expert(e)

        @block.gpsimd
        def _(pool):
            link = Link(pool, pool_link)
            nc.gpsimd.memset(eps_half[:, :], -0.5)
            link(nc.gpsimd.memset(ident[:, :], 0.0))
            nc.gpsimd.affine_select(out=ident[:, :], in_=ident[:, :], compare_op=ALU.not_equal, fill=1.0,
                                         base=0, pattern=[[-1, P]], channel_multiplier=1).then_inc(consts, 1)
            nc.gpsimd.memset(ones_b[:, :], 1.0)
            nc.gpsimd.memset(ones[:, :], 1.0)

            def rstd_x(g):
                sl = slice(g * LDG, (g + 1) * LDG)
                pool.wait_ge(x_stats, g + 1)
                link(nc.gpsimd.tensor_scalar(rs_x[:, sl], mv_x[:, sl, 1], LN_EPS, None, ALU.add))
                nc.gpsimd.tensor_tensor(rs_x[:, sl], rs_x[:, sl], eps_half[:, 0:LDG], ALU.pow).then_inc(x_rstd, 1)

            rstd_x(0)
            nc.gpsimd.memset(tri[:, :], 1.0)
            nc.gpsimd.memset(stri[:, :], 1.0)
            nc.gpsimd.memset(last_row[:, :], 0.0)
            nc.gpsimd.memset(mask[:, :], 0.0)
            link(nc.gpsimd.memset(pad_row[:, :], 0.0))
            nc.gpsimd.affine_select(out=tri[:, :], in_=tri[:, :], compare_op=ALU.is_ge, fill=0.0,
                                    base=0, pattern=[[1, P]], channel_multiplier=-1)
            nc.gpsimd.affine_select(out=stri[:, :], in_=stri[:, :], compare_op=ALU.is_gt, fill=0.0,
                                    base=0, pattern=[[1, P]], channel_multiplier=-1)
            rstd_x(1)
            nc.gpsimd.affine_select(out=last_row[:, :], in_=last_row[:, :], compare_op=ALU.not_equal, fill=1.0,
                                    base=1 - P, pattern=[[0, P]], channel_multiplier=1)
            nc.gpsimd.affine_select(out=mask[:, :], in_=mask[:, :], compare_op=ALU.is_ge, fill=MASKED,
                                    base=0, pattern=[[0, 4], [1, P]], channel_multiplier=-1)
            pool.wait_ge(consts, 1)
            nc.gpsimd.tensor_copy(identb[:, :], ident[:, :])
            nc.gpsimd.iota(pad_row[:, TOKEN:TOKEN + 1].bitcast(U32), pattern=[[0, 1]], base=int(DROPPED),
                           channel_multiplier=0).then_inc(pad_ready, 1)
            nc.gpsimd.iota(token_id[:, :], pattern=[[P, NT]], base=0, channel_multiplier=1)
            nc.gpsimd.iota(iota_e[:, :], pattern=[[1, E]], base=0, channel_multiplier=0,
                           allow_small_or_imprecise_dtypes=True)
            nc.gpsimd.memset(before[:, 0, :], 0.0).then_inc(consts, 1)
            rstd_x(2)
            nc.gpsimd.memset(rows_l[:, :], 1.0).then_inc(rows_set, 1)
            rstd_x(3)
            nc.gpsimd.memset(rows_r[:, :], 1.0).then_inc(rows_set, 1)
            nc.gpsimd.memset(state[:, :, :, :], 0.0)
            nc.gpsimd.memset(q_diag[:, :, :, :, :], 0.0).then_inc(consts, 1)
            link(nc.gpsimd.memset(v_aug[:, :, :], 1.0))
            for g in range(NG):
                pool.wait_ge(c_in[g], 16)
                for t in range(g * LDG, (g + 1) * LDG):
                    nc.gpsimd.tensor_copy(v_aug[:, t, 0:NH * DV].rearrange("p (h n) -> p h n", h=NH)[:, :, 0:DH],
                                          c_all[:, t, :].rearrange("p (h d) -> p h d", h=NH)).then_inc(v_ready, 1)

            def decayed_keys(b):
                if b >= 2:
                    pool.wait_ge(state_done, b - 1)
                if b == 0:
                    pool.wait_ge(factors_ready, 1)
                nc.gpsimd.tensor_tensor(kdec[:, b % 2, :].rearrange("p (h d) -> p h d", h=NH),
                                        c_all[:, 2 * b, :].rearrange("p (h d) -> p h d", h=NH),
                                        kfac[:, b * NH:(b + 1) * NH].unsqueeze(2).broadcast_to([P, NH, DH]),
                                        ALU.mult).then_inc(kdec_ready, 1)

            decayed_keys(0)
            decayed_keys(1)
            for step in range(STEPS + 1):
                if (b := batch_at(step, -3)) is not None and b >= 2:
                    decayed_keys(b)
                if (b := batch_at(step, 2)) is not None:
                    pool.wait_ge(h_stats, b + 1)
                    link(nc.gpsimd.tensor_scalar(rs_h[:, :], mv_h[:, :, 1], LN_EPS, None, ALU.add))
                    nc.gpsimd.tensor_tensor(rs_h[:, :], rs_h[:, :], eps_half[:, 0:2], ALU.pow).then_inc(h_rstd, 1)
                if (b := batch_at(step, 3)) is not None:
                    hh = h_sb[:, b % 2, :, :]
                    pool.wait_ge(h_normed, b + 1)
                    link(nc.gpsimd.tensor_tensor(hh, hh, lns[:, :].unsqueeze(1).broadcast_to([P, 2, D]), ALU.mult))
                    x1 = x_all[:, 2 * b:2 * b + 2, :]
                    nc.gpsimd.tensor_tensor(x1, hh, x1, ALU.add).then_inc(x1_ready, 1)
                if (b := batch_at(step, 4)) is not None:
                    pool.wait_ge(x1_stats, b + 1)
                    link(nc.gpsimd.tensor_scalar(rs_1[:, :], mv_1[:, :, 1], LN_EPS, None, ALU.add))
                    nc.gpsimd.tensor_tensor(rs_1[:, :], rs_1[:, :], eps_half[:, 0:2], ALU.pow).then_inc(x1_rstd, 1)
                b = batch_at(step, 9) if step < UNITS + 1 else batch_at(step, 10)
                if b is not None:
                    pool.wait_ge(placed, b + 1)
                    if b == 0:
                        pool.wait_ge(pads_out, 16)
                    for i in range(2):
                        for k in range(2):
                            c = 2 * i + k
                            nc.gpsimd.indirect_dma_start(
                                slots, bass.IndirectOffsetOnAxis(ap=slot_i[:, b % 2, c:c + 1], axis=0),
                                row[:, b % ROWS, i, :], None, bounds_check=E * CAP - 1, oob_is_err=False,
                            ).then_inc(rows_out[b % 2], 16)

            pool.wait_ge(w_phase, 1)
            nc.gpsimd.memset(acc[:, :, :], 0.0).then_inc(acc_set, 1)
            pool.wait_ge(acc_set, 1)
            pool.wait_ge(x1_out, 16 * NBATCH)
            for e in range(E):
                if e == 0:
                    for t in range(TT):
                        pool.wait_ge(xg_first[t], 16)
                else:
                    pool.wait_ge(xg_in[e % 2], 16 * ((e + 1) // 2))
                pool.wait_ge(b2_in[e % 2], 16 * (e // 2 + 1))
                if e >= 1:
                    pool.wait_ge(res_out, 16 * TT * e)
                    pool.wait_ge(res_ready, TT * e)
                for t in range(TT):
                    nc.gpsimd.indirect_dma_start(
                        acc[:, t, :], None, out_rows,
                        bass.IndirectOffsetOnAxis(ap=xg[:, e % 2, t, TOKEN:TOKEN + 1].bitcast(U32), axis=0),
                        bounds_check=N - 1, oob_is_err=False).then_inc(acc_in, 16)
                pool.wait_ge(weights_ready, e + 1)
                for t in range(TT):
                    last = nc.gpsimd.tensor_scalar(bias_w[:, t, :], b2_b[:, e % 2, :], gate_w[:, e % 2, t:t + 1], None, ALU.mult)
                link(last)
                pool.wait_ge(acc_in, 16 * TT * (e + 1))
                for t in range(TT):
                    nc.gpsimd.tensor_tensor(acc[:, t, :], acc[:, t, :], bias_w[:, t, :], ALU.add).then_inc(acc_ready, 1)
                for t in range(TT):
                    pool.wait_ge(res_ready, TT * e + t + 1)
                    nc.gpsimd.indirect_dma_start(
                        out_rows, bass.IndirectOffsetOnAxis(ap=xg[:, e % 2, t, TOKEN:TOKEN + 1].bitcast(U32), axis=0),
                        res[:, t, :], None, bounds_check=N - 1, oob_is_err=False).then_inc(res_out, 16)
            pool.wait_ge(res_out, 16 * TT * E)

        @block.scalar
        def _(act):
            link = Link(act, act_link)
            act.dma_start(gw[0:NH, :], igate_w).then_inc(small_in, 16)
            act.dma_start(gw[NH:2 * NH, :], fgate_w).then_inc(small_in, 16)
            act.dma_start(gate_b[:, 0:NH], igate_b.rearrange("(a n) -> a n", a=1).broadcast_to([P, NH])).then_inc(small_in, 16)
            act.dma_start(gate_b[:, NH:2 * NH], fgate_b.rearrange("(a n) -> a n", a=1).broadcast_to([P, NH])).then_inc(small_in, 16)
            act.dma_start(b1_raw[:, :], b1.rearrange("e (j p) -> (e j) p", p=P)).then_inc(small_in, 16)
            act.dma_start(wr_sb[:, :, :], Wr.rearrange("(k p) e -> p k e", p=P)).then_inc(small_in, 16)
            act.dma_start(lns[:, :], ln_scale.rearrange("(a n) -> a n", a=1).broadcast_to([P, D])).then_inc(small_in, 16)
            act.dma_start(br_b[:, :], br.rearrange("(a n) -> a n", a=1).broadcast_to([P, E])).then_inc(small_in, 16)

            def gates_copy(g):
                act.wait_ge(gT_done, g + 1)
                if g >= 1:
                    act.wait_ge(gates_done, g)
                nc.scalar.activation(gT[:, :], gate_bank(g), ACT.Copy).then_inc(gT_copied, 1)

            for t in range(NT):
                act.wait_ge(xc_turned, t + 1)
                nc.scalar.activation(xcT[:, t, :, :], turn_bank(t), ACT.Copy).then_inc(xc_copied, 1)
                if t % LDG == 0 and t >= 2 * LDG:
                    gates_copy(t // LDG - 2)
            gates_copy(NG - 2)
            gates_copy(NG - 1)
            act.wait_ge(fabs_ready, 1)
            link(nc.scalar.activation(fabs[:, :, :], fabs[:, :, :], ACT.Exp, scale=-1.0))
            nc.scalar.activation(fabs[:, :, :], fabs[:, :, :], ACT.Ln, bias=1.0).then_inc(softplus_ready, 1)
            act.wait_ge(a_turned, 1)
            nc.scalar.activation(am[:, 0, :], ps_s[0:BH, 0:S], ACT.Copy).then_inc(a_copied, 1)
            act.wait_ge(exps_in, 1)
            nc.scalar.activation(floor_n[:, :, :], floor_n[:, :, :], ACT.Exp, scale=-1.0)
            nc.scalar.activation(qfac[:, :], qfac[:, :], ACT.Exp)
            nc.scalar.activation(kfac[:, :], kfac[:, :], ACT.Exp).then_inc(factors_ready, 1)

            def diag_queries(u):
                if u == 0:
                    act.wait_ge(consts, 3)
                if u >= 2:
                    act.wait_ge(s_done, u - 1)
                for j in range(HPC):
                    last = nc.scalar.activation(q_diag[DH * j:DH * (j + 1), u % 2, :, j, :],
                                                xcT[DH * j:DH * (j + 1), u, 0:KC, :], ACT.Copy)
                    last.then_inc(q_ready, 1)

            diag_queries(0)
            for step in range(STEPS + 1):
                if step < UNITS:
                    act.wait_ge(log_done, step + 1)
                    if step >= 2:
                        act.wait_ge(c_ready, step - 1)
                    nc.scalar.activation(decay[:, step % 2, :], ps_a[:, :], ACT.Exp).then_inc(exp_done, 1)
                if step + 1 < UNITS:
                    diag_queries(step + 1)
                if (b := batch_at(step, 7)) is not None:
                    act.wait_ge(row_turned, b + 1)
                    if b >= 1:
                        act.wait_ge(router_done, b)
                    nc.scalar.activation(rowT[:, :, :], ps_t.rearrange("p (k s) -> p k s", k=KC), ACT.Copy).then_inc(rowT_ready, 1)
                if 0 <= step - 1 < UNITS:
                    act.wait_ge(oT_done, step)
                    if step >= 2:
                        act.wait_ge(o_done, step - 1)
                    nc.scalar.activation(oT_sb[:, :], ps_o[:, :], ACT.Copy).then_inc(oT_copied, 1)
                if (b := batch_at(step, 0)) is not None:
                    act.wait_ge(state_done, b + 1)
                    if b >= 2:
                        act.wait_ge(f_done, b - 1)
                    for j in range(HPC):
                        nc.scalar.activation(
                            state[DH * j:DH * (j + 1), b % 2, :, DV * j:DV * (j + 1)],
                            ps_f[DH * j:DH * (j + 1), 0:KC * HPC * DV].rearrange("p (k n) -> p k n", k=KC)[:, :, DV * j:DV * (j + 1)],
                            ACT.Copy).then_inc(state_ready, 1)
                if (b := batch_at(step, 8)) is not None:
                    act.wait_ge(picked, b + 1)
                    nc.scalar.activation(gexp[:, b % 2, :], gdiff[:, b % 2, :], ACT.Exp).then_inc(gexp_ready, 1)
                if 0 <= (j := step - 1) < PIECES:
                    act.wait_ge(w_in[j], 16)
                    nc.scalar.activation(w_hi[0][:, j, :], w_raw[:, j, :], ACT.Copy).then_inc(w_hi_ready, 1)

            def x_high(e):
                act.wait_ge(xg_turned, e + 1)
                if e >= 2:
                    act.wait_ge(ffn1_done, HJ * (e - 1))
                nc.scalar.activation(x_hi[:, e % 2, :, :], ps_x[:, :].rearrange("p (k s) -> p k s", k=KC), ACT.Copy
                                     ).then_inc(x_hi_ready, 1)

            x_high(0)
            for g in range(E * HJ):
                e, j = divmod(g, HJ)
                act.wait_ge(ffn1_done, g + 1)
                if g >= 3:
                    act.wait_ge(g_lo_ready, g - 2)
                nc.scalar.activation(g_f[:, g % 3, :], ps_s[:, (g % 2) * CAP:(g % 2 + 1) * CAP], ACT.Gelu,
                                     bias=b1_cols[:, g:g + 1]).then_inc(gelu_done, 1)
                if e + 1 < E:
                    act.wait_ge(w_in[j], 16 * (e + 2))
                    if e >= 1:
                        act.wait_ge(ffn1_done, HJ * e) if j < 4 else act.wait_ge(ffn2_done, HJ * e)
                    nc.scalar.activation(w_hi[(e + 1) % 2][:, j, :], w_raw[:, j, :], ACT.Copy).then_inc(w_hi_ready, 1)
                act.wait_ge(gelu_done, g + 1)
                if g >= 3:
                    act.wait_ge(ffn2_done, g - 2)
                nc.scalar.activation(g_hi[:, g % 3, :], g_f[:, g % 3, :], ACT.Copy).then_inc(g_hi_ready, 1)
                if j == 5 and e + 1 < E:
                    x_high(e + 1)

        @block.vector
        def _(dve):
            link = Link(dve, dve_link)
            for g in range(NG):
                dve.wait_ge(x_in[g], 16)
                tiles = range(g * LDG, (g + 1) * LDG)
                for t in tiles:
                    last = nc.vector.bn_stats(stat_x[:, t, :], x_all[:, t, :])
                link(last)
                for t in tiles:
                    last = nc.vector.bn_aggr(mv_x[:, t, :], stat_x[:, t, :])
                last.then_inc(x_stats, 1)
                dve.wait_ge(x_rstd, g + 1)
                for t in tiles:
                    if t >= LDG:
                        dve.wait_ge(xc_turned, t - LDG + 1)
                    nc.vector.tensor_scalar(xn[:, t % LDG, :], x_all[:, t, :], mv_x[:, t, 0:1], rs_x[:, t:t + 1],
                                            ALU.subtract, ALU.mult).then_inc(xn_ready, 1)
                if g == 1:
                    dve.wait_ge(gw_turned, 1)
                    w = 2 * NH
                    nc.vector.tensor_copy(gw_q[:, :, :], ps_t[:, 0:2 * w].rearrange("p (k n) -> p k n", k=KC))
                    nc.vector.tensor_copy(b1_cols[:, :], ps_t[:, 6 * w:6 * w + E * HJ])
                    link(nc.vector.tensor_copy(gw_v[:, :, :], ps_t[:, 4 * w:6 * w].rearrange("p (k n) -> p k n", k=KC)))
                    nc.vector.tensor_tensor(gw_c[:, :, :], ps_t[:, 2 * w:4 * w].rearrange("p (k n) -> p k n", k=KC),
                                            gw_v[:, :, :], ALU.add).then_inc(gw_ready, 1)
            dve.wait_ge(gates_done, NG)
            dve.wait_ge(small_in, 16 * NSMALL)
            link(nc.vector.tensor_tensor(gates[:, :, :], ps_f[:, 0:NT * 2 * NH].rearrange("p (t n) -> p t n", t=NT),
                                         gate_b[:, :].unsqueeze(1).broadcast_to([P, NT, 2 * NH]), ALU.add))
            nc.vector.scalar_tensor_tensor(out=fabs[:, :, :], in0=gates[:, :, NH:2 * NH], scalar=-1.0,
                                           in1=gates[:, :, NH:2 * NH], op0=ALU.mult, op1=ALU.max).then_inc(fabs_ready, 1)
            dve.wait_ge(softplus_ready, 1)
            nc.vector.scalar_tensor_tensor(out=logf[:, :, :], in0=gates[:, :, NH:2 * NH], scalar=0.0, in1=fabs[:, :, :],
                                           op0=ALU.min, op1=ALU.subtract).then_inc(logf_ready, 1)
            dve.wait_ge(csum_done, 1)
            for i in range(2):
                last = nc.vector.tensor_copy(csum[:, i, :].rearrange("p (b h) -> p b h", b=NBATCH),
                                             ps_t[:, 0:NT * NH].rearrange("p (b i h) -> p b i h", i=2, h=NH)[:, :, i, :])
            link(last)
            for i in range(2):
                last = nc.vector.tensor_tensor(acol[:, i, :].rearrange("p (b h) -> p b h", b=NBATCH),
                                               gates[:, :, 0:NH].rearrange("p (b i) h -> p b i h", i=2)[:, :, i, :],
                                               csum[:, i, :].rearrange("p (b h) -> p b h", b=NBATCH), ALU.subtract)
            last.then_inc(acol_ready, 1)
            dve.wait_ge(a_copied, 1)
            nc.vector.tensor_tensor_scan(mrow[:, :], am[:, 0, :], am[:, 0, :], -3.0e38, ALU.max, ALU.max).then_inc(m_scanned, 1)
            dve.wait_ge(m_scanned, 1)
            link(nc.vector.tensor_scalar(am[:, 1, :], mrow[:, :], -1.0, None, ALU.mult))
            for k in range(3):
                nc.vector.tensor_copy(part[k][:, :, :], am[:, :, :]).then_inc(parts_ready, 1)
                dve.wait_ge(parts_ready, k + 1)
                if k < 2:
                    link(nc.vector.tensor_tensor(am[:, :, :], am[:, :, :], part[k][:, :, :], ALU.subtract))
            dve.wait_ge(m_turned, 1)
            link(nc.vector.tensor_copy(mtok[:, :, :], ps_s[:, 0:2 * BH].rearrange("p (i n) -> p i n", i=2)))
            nc.vector.tensor_tensor(floor_n[:, :, :], csum[:, :, :], mtok[:, :, :], ALU.add).then_inc(mtok_ready, 1)
            dve.wait_ge(ref_ready, 1)
            nc.vector.tensor_tensor(qfac[:, :], ps_o[:, 0:BH], mtok[:, 1, :], ALU.subtract)
            nc.vector.scalar_tensor_tensor(out=kfac[:, :], in0=ps_o[:, 0:BH], scalar=-1.0, in1=acol[:, 0, :],
                                           op0=ALU.mult, op1=ALU.add).then_inc(exps_in, 1)

            for step in range(STEPS + 1):
                if (b := batch_at(step, 2)) is not None:
                    if b == 0:
                        dve.wait_ge(factors_ready, 1)
                    dve.wait_ge(f_done, b + 1)
                    nc.vector.tensor_tensor(f_sb[:, :].rearrange("p (h n) -> p h n", h=NH),
                                            ps_f[:, 0:NH * DV].rearrange("p (h n) -> p h n", h=NH),
                                            qfac[:, b * NH:(b + 1) * NH].unsqueeze(2).broadcast_to([P, NH, DV]),
                                            ALU.mult).then_inc(f_taken, 1)
                if step < UNITS:
                    u = step
                    dve.wait_ge(s_done, u + 1)
                    dve.wait_ge(exp_done, u + 1)
                    if u >= 2:
                        dve.wait_ge(oT_done, u - 1)
                    nc.vector.tensor_tensor(cmat[:, u % 2, :], ps_s[:, :], decay[:, u % 2, :], ALU.mult).then_inc(c_ready, 1)
                u = step - 1
                if 0 <= u < UNITS:
                    b, i = divmod(u, 2)
                    dve.wait_ge(o_done, u + 1)
                    sums = ps_t.rearrange("p (h n) -> p h n", h=NH)[:, :, 0:DV]
                    if i == 0:
                        nc.vector.tensor_copy(o_sb[:, 0, :].rearrange("p (h n) -> p h n", h=NH), sums).then_inc(o_taken, 1)
                    else:
                        dve.wait_ge(f_taken, b + 1)
                        nc.vector.tensor_tensor(o_sb[:, 1, :].rearrange("p (h n) -> p h n", h=NH), sums,
                                                f_sb[:, :].rearrange("p (h n) -> p h n", h=NH), ALU.add).then_inc(o_taken, 1)
                if (b := batch_at(step, 2)) is not None:
                    hh = h_sb[:, b % 2, :, :]
                    osb = o_sb[:, :, :].rearrange("p i (h n) -> p i h n", h=NH)
                    fl = floor_n[:, :, b * NH:(b + 1) * NH]
                    dve.wait_ge(o_taken, 2 * b + 2)
                    link(nc.vector.scalar_tensor_tensor(out=den[:, :, :], in0=osb[:, :, :, DH], scalar=-1.0,
                                                        in1=osb[:, :, :, DH], op0=ALU.mult, op1=ALU.max))
                    link(nc.vector.scalar_tensor_tensor(out=den[:, :, :], in0=den[:, :, :], scalar=SCALE, in1=fl,
                                                        op0=ALU.mult, op1=ALU.max))
                    link(nc.vector.tensor_scalar(den[:, :, :], den[:, :, :], NORM_EPS, 1.0 / SCALE, ALU.add, ALU.mult))
                    link(nc.vector.reciprocal(den[:, :, :], den[:, :, :]))
                    if b >= 2:
                        dve.wait_ge(x1_ready, b - 1)
                    for i in range(2):
                        last = nc.vector.tensor_tensor(hh[:, i, :].rearrange("p (h d) -> p h d", h=NH), osb[:, i, :, 0:DH],
                                                       den[:, i, :].unsqueeze(2).broadcast_to([P, NH, DH]), ALU.mult)
                    link(last)
                    for i in range(2):
                        last = nc.vector.bn_stats(stat[:, i, :], hh[:, i, :])
                    link(last)
                    for i in range(2):
                        last = nc.vector.bn_aggr(mv_h[:, i, :], stat[:, i, :])
                    last.then_inc(h_stats, 1)
                if (b := batch_at(step, 3)) is not None:
                    hh = h_sb[:, b % 2, :, :]
                    dve.wait_ge(h_rstd, b + 1)
                    for i in range(2):
                        last = nc.vector.tensor_scalar(hh[:, i, :], hh[:, i, :], mv_h[:, i, 0:1], rs_h[:, i:i + 1],
                                                       ALU.subtract, ALU.mult)
                    last.then_inc(h_normed, 1)
                if (b := batch_at(step, 4)) is not None:
                    dve.wait_ge(x1_ready, b + 1)
                    for i in range(2):
                        last = nc.vector.bn_stats(stat_1[:, i, :], x_all[:, 2 * b + i, :])
                    link(last)
                    for i in range(2):
                        last = nc.vector.bn_aggr(mv_1[:, i, :], stat_1[:, i, :])
                    last.then_inc(x1_stats, 1)
                if (b := batch_at(step, 5)) is not None:
                    dve.wait_ge(x1_rstd, b + 1)
                    if b >= ROWS:
                        dve.wait_ge(rows_out[(b - ROWS) % 2], 64 * ((b - ROWS) // 2 + 1))
                    for i in range(2):
                        last = nc.vector.tensor_scalar(row[:, b % ROWS, i, 0:D], x_all[:, 2 * b + i, :], mv_1[:, i, 0:1],
                                                       rs_1[:, i:i + 1], ALU.subtract, ALU.mult)
                    last.then_inc(row_ready, 1)
                if (b := batch_at(step, 9)) is not None:
                    dve.wait_ge(router_done, min(b + 2, NBATCH + 1))
                    nc.vector.tensor_tensor(hotrank[:, :, :, :], hot[:, b % 2, :, :, :],
                                                 ps_r[:, 64:64 + 2 * E].rearrange("p (i e) -> p i e", i=2).unsqueeze(2)
                                                 .broadcast_to([P, 2, 2, E]), ALU.mult).then_inc(hot_ranked, 1)
                if (b := batch_at(step, 7)) is not None:
                    dve.wait_ge(router_done, b + 1)
                    if b >= 2:
                        dve.wait_ge(gexp_ready, b - 1)
                        dve.wait_ge(placed, b - 1)
                    link(nc.vector.tensor_tensor(logits[:, :, :], ps_r[:, 0:2 * E].rearrange("p (i e) -> p i e", i=2),
                                                 br_b[:, :].unsqueeze(1).broadcast_to([P, 2, E]), ALU.add))
                    for i in range(2):
                        last = nc.vector.max(top[:, i, :], logits[:, i, :])
                    link(last)
                    for i in range(2):
                        last = nc.vector.max_index(topi[:, i, :], top[:, i, :], logits[:, i, :])
                    nc.vector.tensor_tensor(gdiff[:, b % 2, :], top[:, :, 1], top[:, :, 0], ALU.subtract)
                    link(last)
                    link(nc.vector.tensor_copy(topf[:, b % 2, :, :], topi[:, :, 0:2]))
                    link(nc.vector.tensor_tensor(hot[:, b % 2, :, :, :],
                                                 iota_e[:, :].unsqueeze(1).unsqueeze(1).broadcast_to([P, 2, 2, E]),
                                                 topf[:, b % 2, :, :].unsqueeze(3).broadcast_to([P, 2, 2, E]), ALU.is_equal))
                    link(nc.vector.tensor_tensor(sel[:, :, :], hot[:, b % 2, :, 0, :], hot[:, b % 2, :, 1, :], ALU.add))
                    link(nc.vector.tensor_tensor(before[:, 2 * b + 1, :], before[:, 2 * b, :], sel[:, 0, :], ALU.add))
                    nc.vector.tensor_tensor(before[:, 2 * b + 2, :], before[:, 2 * b + 1, :], sel[:, 1, :], ALU.add
                                            ).then_inc(picked, 1)
                if (b := batch_at(step, 9)) is not None:
                    dve.wait_ge(hot_ranked, b + 1)
                    link(nc.vector.tensor_reduce(rank[:, :, :], hotrank[:, :, :, :], AX_X, ALU.add))
                    nc.vector.tensor_scalar(over[:, :, :], rank[:, :, :], float(CAP), DROPPED, ALU.is_ge, ALU.mult)
                    link(nc.vector.scalar_tensor_tensor(out=slot_f[:, :, :], in0=topf[:, b % 2, :, :], scalar=float(CAP),
                                                        in1=rank[:, :, :], op0=ALU.mult, op1=ALU.add))
                    if b >= 2:
                        dve.wait_ge(rows_out[b % 2], 64 * (b // 2))
                    nc.vector.tensor_tensor(slot_i[:, b % 2, :].rearrange("p (i k) -> p i k", i=2), slot_f[:, :, :],
                                            over[:, :, :], ALU.add)
                    dve.wait_ge(gexp_ready, b + 1)
                    rw = row[:, b % ROWS, :, :]
                    link(nc.vector.tensor_scalar(gdiff[:, b % 2, :], gexp[:, b % 2, :], 1.0, None, ALU.add))
                    link(nc.vector.reciprocal(rw[:, :, GATE], gdiff[:, b % 2, :]))
                    nc.vector.tensor_tensor(rw[:, :, GATE + 1], gexp[:, b % 2, :], rw[:, :, GATE], ALU.mult)
                    nc.vector.tensor_copy(rw[:, :, FIRST], topf[:, b % 2, :, 0])
                    nc.vector.tensor_copy(rw[:, :, TOKEN].bitcast(U32), token_id[:, 2 * b:2 * b + 2]).then_inc(placed, 1)
                if 0 <= (j := step - 2) < PIECES:
                    dve.wait_ge(w_hi_ready, j + 1)
                    nc.vector.tensor_tensor(w_lo[0][:, j, :], w_raw[:, j, :], w_hi[0][:, j, :].bitcast(F32), ALU.subtract
                                            ).then_inc(w_lo_ready, 1)
            dve.wait_ge(placed, NBATCH)
            nc.vector.memset(gate_w[:, :, :], 0.0).then_inc(w_phase, 1)
            dve.wait_ge(w_phase, 1)

            def x_low(e):
                dve.wait_ge(x_hi_ready, e + 1)
                nc.vector.tensor_tensor(x_lo[:, e % 2, :, :], ps_x[:, :].rearrange("p (k s) -> p k s", k=KC),
                                        x_hi[:, e % 2, :, :].bitcast(F32), ALU.subtract).then_inc(x_lo_ready, 1)

            def slot_weights(e):
                s = e % 2
                if e == 0:
                    for t in range(TT):
                        dve.wait_ge(xg_first[t], 16)
                else:
                    dve.wait_ge(xg_in[s], 16 * ((e + 1) // 2))
                nc.vector.scalar_tensor_tensor(out=gate_w[:, s, :], in0=xg[:, s, :, FIRST], scalar=float(e),
                                               in1=xg[:, s, :, GATE], op0=ALU.is_equal, op1=ALU.mult)
                link(nc.vector.scalar_tensor_tensor(out=gate_2[:, s, :], in0=xg[:, s, :, FIRST], scalar=float(e),
                                                    in1=xg[:, s, :, GATE + 1], op0=ALU.not_equal, op1=ALU.mult))
                nc.vector.tensor_tensor(gate_w[:, s, :], gate_w[:, s, :], gate_2[:, s, :], ALU.add).then_inc(weights_ready, 1)

            def results(e):
                for t in range(TT):
                    if t == 0:
                        dve.wait_ge(ffn2_done, HJ * (e + 1))
                        if e >= 1:
                            dve.wait_ge(res_out, 16 * TT * e)
                    dve.wait_ge(acc_ready, TT * e + t + 1)
                    nc.vector.scalar_tensor_tensor(out=res[:, t, :], in0=out_bank(t), scalar=gate_w[:, e % 2, t:t + 1],
                                                   in1=acc[:, t, :], op0=ALU.mult, op1=ALU.add).then_inc(res_ready, 1)

            x_low(0)
            slot_weights(0)
            for g in range(E * HJ):
                e, j = divmod(g, HJ)
                if e + 1 < E:
                    dve.wait_ge(w_hi_ready, PIECES * (e + 1) + j + 1)
                    nc.vector.tensor_tensor(w_lo[(e + 1) % 2][:, j, :], w_raw[:, j, :], w_hi[(e + 1) % 2][:, j, :].bitcast(F32),
                                            ALU.subtract).then_inc(w_lo_ready, 1)
                if j == 1 and e >= 1:
                    results(e - 1)
                dve.wait_ge(g_hi_ready, g + 1)
                if g >= 3:
                    dve.wait_ge(ffn2_done, g - 2)
                nc.vector.tensor_tensor(g_lo[:, g % 3, :], g_f[:, g % 3, :], g_hi[:, g % 3, :].bitcast(F32), ALU.subtract
                                        ).then_inc(g_lo_ready, 1)
                if j == 5 and e + 1 < E:
                    x_low(e + 1)
                    slot_weights(e + 1)
            results(E - 1)

        @block.tensor
        def _(pe):
            mm = nc.tensor.matmul
            pe.wait_ge(consts, 1)
            w = 2 * NH

            def turn_weights():
                pe.wait_ge(small_in, 16 * NSMALL)
                for c in range(6):
                    nc.tensor.transpose(ps_t[:, c * w:(c + 1) * w], gw[:, c * P:(c + 1) * P], ident[0:w, 0:w])
                nc.tensor.transpose(ps_t[:, 6 * w:6 * w + E * HJ], b1_raw[:, :], ident[0:E * HJ, 0:E * HJ]
                                    ).then_inc(gw_turned, 1)

            def turn(t):
                pe.wait_ge(xn_ready, t + 1)
                pe.wait_ge(c_in[t // LDG], 16)
                if t >= 4:
                    pe.wait_ge(xc_copied, t - 3)
                bank = turn_bank(t)
                for k in range(KC):
                    nc.tensor.transpose(bank[:, (KC + k) * P:(KC + k + 1) * P], c_all[:, t, k * P:(k + 1) * P], ident[:, :])
                for k in range(KC):
                    last = nc.tensor.transpose(bank[:, k * P:(k + 1) * P], xn[:, t % LDG, k * P:(k + 1) * P], ident[:, :])
                last.then_inc(xc_turned, 1)

            def gate_product(g):
                pe.wait_ge(xc_copied, (g + 1) * LDG)
                if g >= 2:
                    pe.wait_ge(gT_copied, g - 1)
                for c in range(2 * KC):
                    lhs = gw_q[:, c, :] if c < KC else gw_c[:, c - KC, :]
                    last = mm(gate_bank(g), lhs, xcT[:, g * LDG:(g + 1) * LDG, c, :], start=(c == 0), stop=(c == 2 * KC - 1))
                last.then_inc(gT_done, 1)

            def gate_turn(g):
                pe.wait_ge(gT_copied, g + 1)
                for t in range(LDG):
                    last = nc.tensor.transpose(ps_f[:, (g * LDG + t) * w:(g * LDG + t + 1) * w], gT[:, t * P:(t + 1) * P],
                                               ident[0:w, 0:w])
                last.then_inc(gates_done, 1)

            for t in range(NT):
                turn(t)
                if t == 5:
                    turn_weights()
                if t == 2 * LDG - 1:
                    pe.wait_ge(gw_ready, 1)
                if t % LDG == LDG - 1 and t >= LDG:
                    gate_product(t // LDG - 1)
                if t % LDG == 2 and t >= 2 * LDG:
                    gate_turn(t // LDG - 2)
            gate_product(NG - 1)
            gate_turn(NG - 2)
            gate_turn(NG - 1)
            pe.wait_ge(logf_ready, 1)
            pe.wait_ge(consts, 2)
            mm(ps_t[:, 0:NT * NH], tri[:, :], logf[:, :, :].rearrange("p t h -> p (t h)"), start=True, stop=False,
               skip_group_check=True)
            mm(ps_t[:, 0:NT * NH].rearrange("p (b i h) -> p b i h", i=2, h=NH)[:, :, 1, :], ones[:, :],
               logf[:, :, :].rearrange("p (b i) h -> p b i h", i=2)[:, :, 0, :], start=False, stop=True,
               skip_group_check=True).then_inc(csum_done, 1)
            pe.wait_ge(acol_ready, 1)
            for i in range(2):
                last = nc.tensor.transpose(ps_s[0:BH, i * P:(i + 1) * P], acol[:, i, :], ident[:, :])
            last.then_inc(a_turned, 1)
            pe.wait_ge(m_scanned, 1)
            pe.wait_ge(a_copied, 1)
            for i in range(2):
                last = nc.tensor.transpose(ps_s[:, i * BH:(i + 1) * BH], mrow[:, i * P:(i + 1) * P], ident[0:BH, 0:BH])
            last.then_inc(m_turned, 1)
            pe.wait_ge(mtok_ready, 1)
            mm(ps_o[:, 0:BH], last_row[:, :], mtok[:, 0, :], start=True, stop=True).then_inc(ref_ready, 1)

            def log_decay(u):
                b, i = divmod(u, 2)
                if u % (UNITS // 4) == 0:
                    pe.wait_ge(rows_in[u // (UNITS // 4)], 32)
                if u >= 1:
                    pe.wait_ge(exp_done, u)
                for h in range(NH):
                    r, q = divmod(b * NH + h, BH // 4)
                    cols = slice(q * S + i * P, q * S + (i + 1) * P)
                    mm(ps_a[:, h * P:(h + 1) * P], rows_l[32 * r:32 * r + 6, cols], rows_r[32 * r:32 * r + 6, cols],
                       start=(h % 4 == 0), stop=False, skip_group_check=True)
                for n in range(2):
                    last = mm(ps_a[:, n * 512:(n + 1) * 512], identb[:, :], mask[:, :], start=False, stop=True,
                              skip_group_check=True)
                last.then_inc(log_done, 1)

            def scores(u):
                pe.wait_ge(q_ready, HPC * (u + 1))
                if u >= 1:
                    pe.wait_ge(c_ready, u)
                for k in range(KC):
                    last = mm(ps_s[:, k * 512:(k + 1) * 512], xcT[:, u, KC + k, :],
                              q_diag[:, u % 2, k, :, :].rearrange("p j s -> p (j s)"), start=True, stop=True)
                last.then_inc(s_done, 1)

            def attend(u):
                pe.wait_ge(c_ready, u + 1)
                pe.wait_ge(v_ready, u + 1)
                if u >= 1:
                    pe.wait_ge(oT_copied, u)
                for h in range(NH):
                    at, col = OW * (h % 2), (h // 2) * P
                    last = mm(ps_o[at:at + OW, col:col + P], v_aug[:, u, h * DV:h * DV + OW], cmat[:, u % 2, h * P:(h + 1) * P],
                              start=True, stop=True, skip_group_check=True)
                last.then_inc(oT_done, 1)

            def turn_back(u):
                pe.wait_ge(oT_copied, u + 1)
                if u >= 1:
                    pe.wait_ge(o_taken, u)
                turned = (u + 1 - 7) // 2 + 1
                if turned >= 1:
                    pe.wait_ge(rowT_ready, turned)
                for m in range(NH // 2):
                    last = nc.tensor.transpose(ps_t[:, m * P:(m + 1) * P], oT_sb[:, m * P:(m + 1) * P], ident[:, :])
                last.then_inc(o_done, 1)

            for step in range(STEPS + 1):
                if step < UNITS:
                    log_decay(step)
                if (b := batch_at(step, 7)) is not None:
                    pe.wait_ge(row_ready, b + 1)
                    if b >= 1:
                        pe.wait_ge(rowT_ready, b)
                    pe.wait_ge(o_taken, min(step - 1, UNITS))
                    for k in range(KC):
                        for i in range(2):
                            last = nc.tensor.transpose(ps_t[:, (2 * k + i) * P:(2 * k + i + 1) * P],
                                                       row[:, b % ROWS, i, k * P:(k + 1) * P], ident[:, :])
                    last.then_inc(row_turned, 1)
                if 0 <= step - 1 < UNITS:
                    attend(step - 1)
                if step < UNITS:
                    scores(step)
                if 0 <= step - 1 < UNITS:
                    turn_back(step - 1)
                ranked, routed = batch_at(step, 9), batch_at(step, 7)
                if ranked is not None:
                    b = ranked
                    pe.wait_ge(picked, b + 1)
                    for i in range(2):
                        mm(ps_r[:, 64 + i * E:64 + (i + 1) * E], stri[:, :], sel[:, i, :], start=True, stop=False)
                        last = mm(ps_r[:, 64 + i * E:64 + (i + 1) * E], ones_b[:, :], before[:, 2 * b + i, :], start=False, stop=True)
                if routed is not None:
                    b = routed
                    pe.wait_ge(rowT_ready, b + 1)
                    if b >= 1:
                        pe.wait_ge(picked, b)
                    for i in range(2):
                        for k in range(KC):
                            last = mm(ps_r[:, i * E:(i + 1) * E], rowT[:, k, i * P:(i + 1) * P], wr_sb[:, k, :],
                                      start=(k == 0), stop=(k == KC - 1))
                if ranked is not None or routed is not None:
                    last.then_inc(router_done, 1)
                if (b := batch_at(step, 0)) is not None:
                    pe.wait_ge(kdec_ready, b + 1)
                    pe.wait_ge(v_ready, 2 * b + 2)
                    if b >= 1:
                        pe.wait_ge(f_taken, b)
                    for k in range(KC):
                        n = HPC * DV
                        last = mm(ps_f[:, k * n:(k + 1) * n], kdec[:, b % 2, k * P:(k + 1) * P],
                                  v_aug[:, 2 * b, k * n:(k + 1) * n], start=True, stop=True)
                    last.then_inc(state_done, 1)
                if (b := batch_at(step, 1)) is not None:
                    pe.wait_ge(state_ready, HPC * (b + 1))
                    for k in range(KC):
                        n = HPC * DV
                        last = mm(ps_f[:, k * n:(k + 1) * n], xcT[:, 2 * b + 1, k, :], state[:, b % 2, k, :], start=True, stop=True)
                    last.then_inc(f_done, 1)

            def turn_slots(e):
                if e >= 1:
                    pe.wait_ge(xg_in[e % 2], 16 * ((e + 1) // 2))
                if e >= 1:
                    pe.wait_ge(x_lo_ready, e)
                else:
                    pe.wait_ge(placed, NBATCH)
                for t in range(TT):
                    if e == 0:
                        pe.wait_ge(xg_first[t], 16)
                    for k in range(KC):
                        last = nc.tensor.transpose(ps_x[:, k * CAP + t * P:k * CAP + (t + 1) * P],
                                                   xg[:, e % 2, t, k * P:(k + 1) * P], ident[:, :])
                last.then_inc(xg_turned, 1)

            def hidden(g):
                e, j = divmod(g, HJ)
                s = e % 2
                if j == 0:
                    pe.wait_ge(w_lo_ready, PIECES * e + 3)
                    pe.wait_ge(x_lo_ready, e + 1)
                if j == HJ // 2:
                    pe.wait_ge(w_lo_ready, PIECES * e + 4)
                if g >= 2:
                    pe.wait_ge(gelu_done, g - 1)
                bank = ps_s[:, (g % 2) * CAP:(g % 2 + 1) * CAP]
                n = 0
                for k in range(KC):
                    piece, at = 2 * k + j // 4, (j % 4) * P
                    hi, lo = w_hi[s][:, piece, at:at + P], w_lo[s][:, piece, at:at + P]
                    for a, b in ((hi, x_hi), (lo, x_hi), (hi, x_lo)):
                        last = mm(bank, a, b[:, s, k, :], start=(n == 0), stop=(n == 3 * KC - 1))
                        n += 1
                last.then_inc(ffn1_done, 1)

            def output(g):
                e, j = divmod(g, HJ)
                s = e % 2
                piece, at = PIECES // 2 + j // 2, (j % 2) * D
                hi, lo = w_hi[s][:, piece, at:at + D], w_lo[s][:, piece, at:at + D]
                pe.wait_ge(g_lo_ready, g + 1)
                if j % 2 == 0:
                    pe.wait_ge(w_lo_ready, PIECES * e + piece + 1)
                for t in range(TT):
                    if j == 0 and e >= 1:
                        pe.wait_ge(res_ready, TT * (e - 1) + t + 1)
                    cols = slice(t * P, (t + 1) * P)
                    for n, (a, b) in enumerate(((g_hi, hi), (g_hi, lo), (g_lo, hi))):
                        last = mm(out_bank(t), a[:, g % 3, cols], b, start=(j == 0 and n == 0), stop=(j == HJ - 1 and n == 2))
                last.then_inc(ffn2_done, 1)

            turn_slots(0)
            LAG = 2
            for g in range(E * HJ + LAG):
                if g < E * HJ:
                    hidden(g)
                if g >= LAG:
                    output(g - LAG)
                if g % HJ == 5 and g // HJ + 1 < E:
                    turn_slots(g // HJ + 1)




_INS = ["x", "ctx_1024", "L0_xattn_igate_w", "L0_xattn_igate_b", "L0_xattn_fgate_w", "L0_xattn_fgate_b",
        "L0_xattn_ln_scale", "L0_ffn_Wr", "L0_ffn_br", "L0_ffn_W1", "L0_ffn_b1", "L0_ffn_W2", "L0_ffn_b2"]
_OUTS = [((8, 256, 256), "float32")]


def kernel(**inputs):
    import numpy as _np
    import concourse.bacc as _bacc
    from concourse import mybir as _mybir
    from concourse.bass_utils import run_bass_kernel_spmd as _run

    nc = _bacc.Bacc("TRN2", target_bir_lowering=False, num_devices=1)
    arrays, args = {}, []
    for name in _INS:
        a = _np.ascontiguousarray(inputs[name])
        arrays[f"in_{name}_dram"] = a
        args.append(nc.dram_tensor(f"in_{name}_dram", a.shape, _mybir.dt.from_np(a.dtype), kind="ExternalInput").ap())
    for i, (shape, dtype) in enumerate(_OUTS):
        dt = _mybir.dt.from_np(_np.dtype(dtype))
        args.append(nc.dram_tensor(f"out_{i}_dram", shape, dt, kind="ExternalOutput").ap())
    build_program(nc, *args)
    r = _run(nc, [arrays], core_ids=[0])
    got = tuple(r.results[0][f"out_{i}_dram"] for i in range(len(_OUTS)))
    return got[0]
```
